# Optimizing a Trainium2 kernel written in Bass

```python
import numpy as np
import jax
import jax.numpy as jnp

def _softmax(x, axis=-1):
    return jax.nn.softmax(x, axis=axis)

def _gelu(x):
    return jax.nn.gelu(x, approximate=True)

def _silu(x):
    return jax.nn.silu(x)

def _sigmoid(x):
    return jax.nn.sigmoid(x)

def _layernorm(x, axis=-1, eps=1e-05):
    m = jnp.mean(x, axis=axis, keepdims=True)
    v = jnp.var(x, axis=axis, keepdims=True)
    return (x - m) / jnp.sqrt(v + eps)

def _scatter_add(tgt, idx, src, axis=0):
    return tgt.at[idx].add(src)

def _segment_sum(src, seg, n):
    return jax.ops.segment_sum(src, seg, n)
kernel_name = 'mk_gnn_preln_d2_gnn_r64_131bbf'

def setup_inputs(seed: int=0):
    np.random.seed(seed)
    _w = jnp.asarray

    def _rec_inputs():
        import jax
        import jax.numpy as jnp
        _gk = jax.random.key(seed)
        x = -0.0002117 + 1 * jax.random.normal(jax.random.fold_in(_gk, 1), (50000, 256), jnp.float32)
        _s = jax.random.randint(jax.random.fold_in(_gk, 2), (12500,), 0, 50000, jnp.int32)
        _d = jax.random.randint(jax.random.fold_in(_gk, 3), (12500,), 0, 50000, jnp.int32)
        _loop = jnp.arange(50000, dtype=jnp.int32)
        src = jnp.concatenate([_s, _d, _loop])
        dst = jnp.concatenate([_d, _s, _loop])
        _o = jnp.argsort(dst, stable=True)
        src = src[_o]
        dst = dst[_o]
        return (x, src, dst)
    x, src, dst = _rec_inputs()

    def _L0_gnn_setup():
        import jax, jax.numpy as jnp
        import numpy as np
        N_NODES = 100000
        N_EDGES = 25000
        HIDDEN = 256
        N_LAYERS = 2
        key = jax.random.key(seed)
        k = jax.random.split(key, 7)
        x = jax.random.normal(k[0], (N_NODES, HIDDEN), dtype=jnp.float32)
        edge_index = jax.random.randint(k[1], (2, N_EDGES), 0, N_NODES, dtype=jnp.int64)
        s = 1.0 / np.sqrt(HIDDEN)
        W = jax.random.uniform(k[2], (N_LAYERS, HIDDEN, HIDDEN), jnp.float32, -s, s)
        b = jax.random.uniform(k[3], (N_LAYERS, HIDDEN), jnp.float32, -s, s)
        resW = jax.random.uniform(k[4], (HIDDEN, HIDDEN), jnp.float32, -s, s)
        resb = jax.random.uniform(k[5], (HIDDEN,), jnp.float32, -s, s)
        return {'x': x, 'edge_index': edge_index, 'W': W, 'b': b, 'resW': resW, 'resb': resb}
    _L0_gnn_all = _L0_gnn_setup()
    _L0_gnn_in = {k: v for k, v in _L0_gnn_all.items() if k in ('W', 'b', 'resW', 'resb')}
    del _L0_gnn_all

    def _L1_gnn_setup():
        import jax, jax.numpy as jnp
        import numpy as np
        N = 50000
        E = 6250
        D_IN = 256
        D_HID = 256
        D_OUT = 256

        def _sage_conv(x, edge_index, W_l, W_r, b):
            src, dst = (edge_index[0], edge_index[1])
            msgs = x[src]
            agg_sum = jax.ops.segment_sum(msgs, dst, num_segments=x.shape[0])
            deg = jax.ops.segment_sum(jnp.ones((edge_index.shape[1],), x.dtype), dst, num_segments=x.shape[0])
            agg = agg_sum / jnp.maximum(deg, 1.0)[:, None]
            return agg @ W_l + x @ W_r + b
        key = jax.random.key(seed)
        ks = jax.random.split(key, 8)
        x = jax.random.normal(ks[0], (N, D_IN), dtype=jnp.float32)
        edge_index = jax.random.randint(ks[1], (2, E), 0, N, dtype=jnp.int64)

        def glorot(k, fan_in, fan_out):
            lim = float(np.sqrt(6.0 / (fan_in + fan_out)))
            return jax.random.uniform(k, (fan_in, fan_out), jnp.float32, -lim, lim)
        return {'x': x, 'edge_index': edge_index, 'W1_l': glorot(ks[2], D_IN, D_HID), 'W1_r': glorot(ks[3], D_IN, D_HID), 'b1': jnp.zeros((D_HID,), jnp.float32), 'W2_l': glorot(ks[4], D_HID, D_OUT), 'W2_r': glorot(ks[5], D_HID, D_OUT), 'b2': jnp.zeros((D_OUT,), jnp.float32)}
    _L1_gnn_all = _L1_gnn_setup()
    _L1_gnn_in = {k: v for k, v in _L1_gnn_all.items() if k in ('W1_l', 'W1_r', 'b1', 'W2_l', 'W2_r', 'b2')}
    del _L1_gnn_all
    return {'x': x, 'src': src, 'dst': dst, 'L0_gnn_W': _L0_gnn_in['W'], 'L0_gnn_b': _L0_gnn_in['b'], 'L0_gnn_resW': _L0_gnn_in['resW'], 'L0_gnn_resb': _L0_gnn_in['resb'], 'L1_gnn_W1_l': _L1_gnn_in['W1_l'], 'L1_gnn_W1_r': _L1_gnn_in['W1_r'], 'L1_gnn_b1': _L1_gnn_in['b1'], 'L1_gnn_W2_l': _L1_gnn_in['W2_l'], 'L1_gnn_W2_r': _L1_gnn_in['W2_r'], 'L1_gnn_b2': _L1_gnn_in['b2']}

def reference(x, src, dst, L0_gnn_W, L0_gnn_b, L0_gnn_resW, L0_gnn_resb, L1_gnn_W1_l, L1_gnn_W1_r, L1_gnn_b1, L1_gnn_W2_l, L1_gnn_W2_r, L1_gnn_b2):
    import jax
    import jax.numpy as jnp

    def _L0_gnn_ref(x, edge_index, W, b, resW, resb):
        import jax, jax.numpy as jnp
        import numpy as np
        N_NODES = 100000
        N_EDGES = 25000
        HIDDEN = 256
        N_LAYERS = 2
        N = x.shape[0]
        loop = jnp.arange(N, dtype=edge_index.dtype)
        src = jnp.concatenate([edge_index[0], loop])
        dst = jnp.concatenate([edge_index[1], loop])
        ew = jnp.ones(src.shape[0], dtype=x.dtype)
        deg = jax.ops.segment_sum(ew, dst, num_segments=N)
        dis = jnp.where(deg > 0, jax.lax.rsqrt(jnp.where(deg > 0, deg, 1.0)), 0.0)
        norm = dis[src] * ew * dis[dst]
        for l in range(W.shape[0]):
            x_res = x
            h = x @ W[l]
            msg = norm[:, None] * h[src]
            agg = jax.ops.segment_sum(msg, dst, num_segments=N) + b[l]
            x = jax.nn.relu(agg + x_res @ resW + resb)
        return x

    def _L1_gnn_ref(x, edge_index, W1_l, W1_r, b1, W2_l, W2_r, b2):
        import jax, jax.numpy as jnp
        import numpy as np
        N = 50000
        E = 6250
        D_IN = 256
        D_HID = 256
        D_OUT = 256

        def _sage_conv(x, edge_index, W_l, W_r, b):
            src, dst = (edge_index[0], edge_index[1])
            msgs = x[src]
            agg_sum = jax.ops.segment_sum(msgs, dst, num_segments=x.shape[0])
            deg = jax.ops.segment_sum(jnp.ones((edge_index.shape[1],), x.dtype), dst, num_segments=x.shape[0])
            agg = agg_sum / jnp.maximum(deg, 1.0)[:, None]
            return agg @ W_l + x @ W_r + b
        h = _sage_conv(x, edge_index, W1_l, W1_r, b1)
        h = jax.nn.relu(h)
        out = _sage_conv(h, edge_index, W2_l, W2_r, b2)
        return out
    edge_index = jnp.stack([src, dst])
    h = jnp.maximum(_layernorm(x, axis=-1), 0.0)
    x = x + _L0_gnn_ref(h, edge_index, L0_gnn_W, L0_gnn_b, L0_gnn_resW, L0_gnn_resb)
    h = jnp.maximum(_layernorm(x, axis=-1), 0.0)
    x = x + _L1_gnn_ref(h, edge_index, L1_gnn_W1_l, L1_gnn_W1_r, L1_gnn_b1, L1_gnn_W2_l, L1_gnn_W2_r, L1_gnn_b2)
    return x

_drawn_inputs = setup_inputs


def setup_inputs(seed=0):
    import zlib

    import numpy as np

    out = dict(_drawn_inputs(seed))
    spreads = {'L1_gnn_b1': (0.0, 0.1), 'L1_gnn_b2': (0.0, 0.1)}
    factors = {}
    for name, (base, spread) in spreads.items():
        noise = np.random.default_rng([zlib.crc32(name.encode()), seed]).standard_normal(out[name].shape)
        drawn = base * np.exp(spread * noise) if base else spread * noise
        out[name] = jnp.asarray(drawn.astype(out[name].dtype))
    for name, factor in factors.items():
        out[name] = (out[name] * factor).astype(out[name].dtype)
    return out
```

```python
from contextlib import ExitStack

import concourse.bass as bass
from concourse import mybir

P = 128
D = 256
DC = D // P
GT = 4
ST = 8
WIN = 3
EPS = 1e-5
NF = 8
SLOT, SELF_G, DIS2, SELF_S, INV, DIS, SQ = range(7)
FAR = 1048576.0

F32 = mybir.dt.float32
I32 = mybir.dt.int32
BF16 = mybir.dt.bfloat16
ALU = mybir.AluOpType
ACT = mybir.ActivationFunctionType
AX = mybir.AxisListType
ds = bass.ds


def ceil_div(a, b):
    return -(-a // b)


def gnn_kernel(nc, x, src, dst, gcn_w, gcn_b, res_w, res_b, sage1_l, sage1_r, sage1_b, sage2_l, sage2_r, sage2_b, out):
    N = x.shape[0]
    E = src.shape[0]
    NS = ceil_div(N, ST * P)
    T = NS * ST
    NQ = NS * 2
    NP = T * P
    K = ceil_div(E, P)
    KB = ceil_div(K + WIN, P)
    KP = KB * P
    PAD = T * P
    TB = ceil_div(T, P)
    TW = TB * P
    assert x.shape[1] == D and NS >= 4 and N > (NS - 1) * ST * P

    node_rows = [nc.dram_tensor(f"node_rows_{i}", [NP, D], F32).ap() for i in range(4)]
    sum_rows = nc.dram_tensor("sum_rows", [NP, D], F32).ap()
    x2_rows = nc.dram_tensor("x2_rows", [NP, D], F32).ap()
    edge_table = nc.dram_tensor("edge_table", [KP, 3 * P], F32).ap()
    chunk_rows = nc.dram_tensor("chunk_rows", [3, KP], F32).ap()

    with ExitStack() as ctx:
        def sb(name, shape, dt=F32):
            return ctx.enter_context(nc.sbuf_tensor(name, shape, dt))

        def psum(name):
            return ctx.enter_context(nc.psum_tensor(name, [P, 512], F32))

        def sem(name):
            return ctx.enter_context(nc.semaphore(name))

        own = sb("own", [P, 2, GT, D])
        assert TB * WIN * 4 * P <= 6 * GT * D
        shared = sb("shared", [P, 6 * GT * D])
        resid, done_rows, normed = (
            shared[:, i * 2 * GT * D:(i + 1) * 2 * GT * D].rearrange("p (h j d) -> p h j d", h=2, j=GT) for i in range(3))
        window = shared[:, 0:TB * WIN * 3 * P].rearrange("p (t w f) -> p t w f", t=TB, w=WIN)
        own_loop = shared[:, TB * WIN * 3 * P:TB * WIN * 4 * P].rearrange("p (t w e) -> p t w e", t=TB, w=WIN)
        neigh = sb("neigh", [P, ST, D])
        selfpart = sb("selfpart", [P, 4, D])
        agg = sb("agg", [P, 2, D])
        turned = sb("turned", [P, 2, 2 * D])
        pick = sb("pick", [P, 4, P])
        scal = sb("scal", [P, 2, GT, NF])
        idx_now = sb("idx_now", [P, 2, GT], I32)
        weights = sb("weights", [P, 7, DC, D])
        bias = sb("bias", [P, 4, D])
        res_bias = sb("res_bias", [P, D])
        stat6 = sb("stat6", [P, 2, GT, 6])
        ln_mean = sb("ln_mean", [P, 2, GT])
        ln_diff = sb("ln_diff", [P, 2, GT])
        ln_var = sb("ln_var", [P, 2, GT])
        ln_base = sb("ln_base", [P, 2, 2, GT])
        ln_root = sb("ln_root", [P, 2, 2, GT])
        power = sb("power", [P, 2, GT])
        ln_scale = sb("ln_scale", [P, 2, GT])
        ln_shift = sb("ln_shift", [P, 2, GT])
        table = sb("table", [P, T, NF])
        src_row = sb("src_row", [P, T], I32)

        iota_i = sb("iota_i", [P, P], I32)
        part_i = sb("part_i", [P, 1], I32)
        first_i = sb("first_i", [P, TW], I32)
        iota = sb("iota", [P, P])
        iota16 = sb("iota16", [P, P], BF16)
        part = sb("part", [P, 1])
        first_node = sb("first_node", [P, TW])
        my_first = sb("my_first", [P, TB])
        my_first_i = sb("my_first_i", [P, TB], I32)
        ident = sb("ident", [P, P])
        before = sb("before", [P, P])
        ones = sb("ones", [P, P])

        assert 2 * WIN * TW <= 7 * KP
        edge_scratch = sb("edge_scratch", [P, 7 * KP], I32)

        def scratch(i, dt):
            part_of = edge_scratch[:, i * KP:(i + 1) * KP]
            return (part_of if dt == I32 else part_of.bitcast(dt)).rearrange("p (b e) -> p b e", b=KB)

        dst_i = scratch(0, I32)
        src_i = scratch(1, I32)
        prev_i = scratch(2, I32)
        edges = sb("edges", [P, KB, 3, P])
        tile_of = scratch(3, F32)
        notself = sb("notself", [P, KB, P])
        work = scratch(4, F32)
        rank = scratch(5, F32)
        lead = scratch(6, F32)
        small = sb("small", [P, 3, KB])
        totals = sb("totals", [P, 4, KB])
        chunk_row = sb("chunk_row", [P, 3, KP])
        carried = sb("carried", [P, KP + 1])
        lo = sb("lo", [P, 3, TB])
        lo_i = sb("lo_i", [P, WIN, TB], I32)
        win_t = sb("win_t", [P, 4, WIN, TW])
        win_i, win_j = (edge_scratch[:, i * WIN * TW:(i + 1) * WIN * TW].rearrange("p (w t) -> p w t", w=WIN)
                        for i in range(2))
        facts = sb("facts", [P, WIN, TW, 5], BF16)
        key_now = sb("key_now", [P, 2, 2 * WIN, GT], BF16)
        facts_now = sb("facts_now", [P, 2, WIN, GT, 5], BF16)
        hits = sb("hits", [P, 4, 2 * WIN, P], BF16)
        found = sb("found", [P, T, 5])
        counted = sb("counted", [P, T, 2])
        bad = sb("bad", [P, 4])
        general = sb("general", [P, 2])
        general_i = sb("general_i", [P, 1], I32)
        tmp_a = sb("tmp_a", [P, T])
        tmp_b = sb("tmp_b", [P, T])
        tmp_c = sb("tmp_c", [P, T])
        all_src = sb("all_src", [P, KP])
        all_src_i = sb("all_src_i", [P, KP], I32)
        all_dst = sb("all_dst", [P, KP])
        all_dst_ns = sb("all_dst_ns", [P, KP])
        all_self = sb("all_self", [P, KP])
        slow_first = sb("slow_first", [P, 1])
        slow_idx = sb("slow_idx", [P, 1], I32)
        slow_rhs = sb("slow_rhs", [P, 2])
        counted_now = sb("counted_now", [P, 2])

        ps_agg = [psum("ps_agg0"), psum("ps_agg1")]
        ps_turn = [psum("ps_turn0"), psum("ps_turn1")]
        ps_out = [psum("ps_out0"), psum("ps_out1")]
        ps_prep = [psum("ps_prep0"), psum("ps_prep1")]

        iotas_made = sem("iotas_made")
        pads_set = sem("pads_set")
        edges_loaded = sem("edges_loaded")
        weights_loaded = sem("weights_loaded")
        prep_dve = sem("prep_dve")
        counts_ready = sem("counts_ready")
        bases_ready = sem("bases_ready")
        small_ready = sem("small_ready")
        rows_written = sem("rows_written")
        rows_loaded = sem("rows_loaded")
        edges_ready = sem("edges_ready")
        edges_stored = sem("edges_stored")
        lo_ready = sem("lo_ready")
        window_loaded = sem("window_loaded")
        window_ready = sem("window_ready")
        win_turned = sem("win_turned")
        win_copied = sem("win_copied")
        bad_ready = sem("bad_ready")
        bad_summed = sem("bad_summed")
        flag_ready = sem("flag_ready")
        hits_ready = sem("hits_ready")
        facts_summed = sem("facts_summed")
        facts_copied = sem("facts_copied")
        counts_final = sem("counts_final")
        degrees_ready = sem("degrees_ready")
        table_ready = sem("table_ready")
        buffers_clear = sem("buffers_clear")
        slow_mm_wanted = sem("slow_mm_wanted")
        slow_mm_done = sem("slow_mm_done")
        slow_dve = sem("slow_dve")
        slow_pool = sem("slow_pool")
        slow_gathered = sem("slow_gathered")
        slow_rows_ready = sem("slow_rows_ready")
        slow_next = sem("slow_next")
        slow_sum_ready = sem("slow_sum_ready")
        slow_stored = sem("slow_stored")
        slow_sum_free = sem("slow_sum_free")
        slow_turned = sem("slow_turned")
        slow_turn_copied = sem("slow_turn_copied")
        own_loaded = [sem("own_loaded0"), sem("own_loaded1")]
        resid_loaded = [sem("resid_loaded0"), sem("resid_loaded1")]
        rows_stored = [sem("rows_stored0"), sem("rows_stored1")]
        normed_stored = [sem("normed_stored0"), sem("normed_stored1")]
        gathered = [sem(f"gathered{j}") for j in range(ST)]
        gather_issued = sem("gather_issued")
        idx_copied = sem("idx_copied")
        scal_ready = sem("scal_ready")
        pick_ready = sem("pick_ready")
        self_ready = sem("self_ready")
        agg_done = sem("agg_done")
        combined = sem("combined")
        turn_done = sem("turn_done")
        turned_ready = sem("turned_ready")
        product_done = sem("product_done")
        out_read = sem("out_read")
        out_ready = sem("out_ready")
        stats_ready = sem("stats_ready")
        pool_step = sem("pool_step")
        ln_ready = sem("ln_ready")
        ln_applied = sem("ln_applied")

        def last_rows(h):
            return min(max(N - (NS - 1) * ST * P - h * GT * P, 0), GT * P)

        def last_dmas(h):
            r = last_rows(h)
            return (r >= P) + (r % P > 0)

        def group_of(rows, s, h):
            return rows[ds(s * (ST * P) + h * GT * P, GT * P), :].rearrange("(j p) d -> p j d", p=P)

        def short_group(rows, h):
            at, r = ((NS - 1) * ST + h * GT) * P, last_rows(h)
            full, rest = r // P, r % P
            pieces = []
            if full:
                pieces.append((rows[at:at + full * P, :].rearrange("(j p) d -> p j d", p=P), (0, full), P))
            if rest:
                pieces.append((rows[at + full * P:at + r, :].rearrange("(j p) d -> p j d", j=1), (full, full + 1), rest))
            return pieces

        def own_count(phase, s, h):
            n = phase * NS * 16 + (s + 1) * 16
            if phase > 0 or (isinstance(s, int) and s == NS - 1):
                n = n + (last_dmas(h) - 1) * 16
            return n

        def resid_count(layer, s, h):
            n = (NS if layer == 4 else 0) * 16 + (s + 1) * 16
            if layer == 4 or (isinstance(s, int) and s == NS - 1):
                n = n + (last_dmas(h) - 1) * 16
            return n

        def super_groups(eng):
            yield 0
            with eng.Fori(1, NS) as s:
                yield s

        def super_groups_last(eng):
            yield 0
            with eng.Fori(1, NS - 1) as s:
                yield s
            yield NS - 1

        def tile_steps(eng, ahead, first):
            for j in range(-ahead, ST if first else 0):
                yield 0, j
            with eng.Fori(1 if first else 0, NS - 1) as s:
                for j in range(ST):
                    yield s, j
            for j in range(ST):
                yield NS - 1, j

        def at(s, j, k):
            if j + k < 0 or (isinstance(s, int) and s == NS - 1 and j + k >= ST):
                return None
            i = j + k
            return s + i // ST, i % ST

        def wait_free(eng, semaphore, value):
            if not (isinstance(value, int) and value <= 0):
                eng.wait_ge(semaphore, value)

        edge_pieces = []
        for pair, shift in (((src_i, src), 0), ((dst_i, dst), 0), ((prev_i, dst), 1)):
            for b in range(KB):
                first, row = b * P * P - shift, 0
                if first < 0:
                    edge_pieces.append((pair, (0, 1), 0, 0, P - shift, shift))
                    first, row = P - shift, 1
                full = min(P - row, max(E - first, 0) // P)
                if full:
                    edge_pieces.append((pair, (row, row + full), first, b, P, 0))
                rest = min(E - first - full * P, P)
                if row + full < P and rest > 0:
                    edge_pieces.append((pair, (row + full, row + full + 1), first + full * P, b, rest, 0))

        block = ctx.enter_context(nc.Block())

        @block.sync
        def _(sp):
            sp.wait_ge(pads_set, 1)
            for flat, rows, first, b, width, skip in edge_pieces:
                n = width if rows[1] - rows[0] == 1 else P
                count = (rows[1] - rows[0] - 1) * P + n
                sp.dma_start(flat[0][rows[0]:rows[1], b, skip:skip + n],
                             flat[1][first:first + count].rearrange("(p e) -> p e", e=n)).then_inc(edges_loaded, 16)
            mats = [gcn_w[0], gcn_w[1], res_w, sage1_l, sage1_r, sage2_l, sage2_r]
            for i, m in enumerate(mats):
                sp.dma_start(weights[:, i], m.rearrange("(c p) n -> p c n", p=P)).then_inc(weights_loaded, 16)
            biases = [gcn_b[0], gcn_b[1], sage1_b, sage2_b]
            for i, v in enumerate(biases):
                sp.dma_start(bias[:, i], v.partition_broadcast(P)).then_inc(weights_loaded, 16)
            sp.dma_start(res_bias[:], res_b.partition_broadcast(P)).then_inc(weights_loaded, 16)

            sp.wait_ge(small_ready, 1)
            with nc.allow_non_contiguous_dma("a few values for each chunk"):
                sp.dma_start(chunk_rows.rearrange("c (b p) -> p c b", p=P), small[:]).then_inc(rows_written, 16)
            sp.wait_ge(rows_written, 16)
            sp.dma_start(chunk_row[:].rearrange("p c k -> p (c k)"),
                         chunk_rows.rearrange("c k -> (c k)").partition_broadcast(P)).then_inc(rows_loaded, 16)
            sp.wait_ge(edges_ready, 1)
            sp.dma_start(edge_table.rearrange("(b p) f -> p b f", p=P),
                         edges[:].rearrange("p b c e -> p b (c e)")).then_inc(edges_stored, 16)

            for s in super_groups_last(sp):
                for h in range(2):
                    wait_free(sp, ln_applied, (s * 2 + h - 1) * GT)
                    if isinstance(s, int) and s == NS - 1:
                        for rows, (t0, t1), parts in short_group(x, h):
                            sp.dma_start(own[0:parts, h, t0:t1], rows).then_inc(own_loaded[h], 16)
                    else:
                        sp.dma_start(own[:, h], group_of(x, s, h)).then_inc(own_loaded[h], 16)

            for layer in range(1, 5):
                base = (layer - 1) * T
                if layer in (1, 3):
                    for h in range(2):
                        sp.wait_ge(normed_stored[h], 16 * NS * (1 if layer == 1 else 2))
                else:
                    for h in range(2):
                        sp.wait_ge(rows_stored[h], 16 * NS * (layer - 1))
                for s in super_groups_last(sp):
                    for h in range(2):
                        if not (isinstance(s, int) and s == 0):
                            sp.wait_ge(turn_done, base + (s * 2 + h - 1) * GT)
                            sp.wait_ge(self_ready, base + (s * 2 + h - 1) * GT)
                        sp.dma_start(own[:, h], group_of(node_rows[layer - 1], s, h)).then_inc(own_loaded[h], 16)
                        if layer in (2, 4):
                            if not (isinstance(s, int) and s == 0):
                                sp.wait_ge(out_ready, (layer - 1) * NQ + s * 2 + h - 1)
                            if layer == 4:
                                sp.dma_start(resid[:, h], group_of(x2_rows, s, h)).then_inc(resid_loaded[h], 16)
                            elif isinstance(s, int) and s == NS - 1:
                                for rows, (t0, t1), parts in short_group(x, h):
                                    sp.dma_start(resid[0:parts, h, t0:t1], rows).then_inc(resid_loaded[h], 16)
                            else:
                                sp.dma_start(resid[:, h], group_of(x, s, h)).then_inc(resid_loaded[h], 16)

        @block.gpsimd
        def _(pool):
            nc.gpsimd.iota(iota_i[:], [[1, P]], base=0, channel_multiplier=0)
            nc.gpsimd.iota(part_i[:], [[0, 1]], base=0, channel_multiplier=1)
            nc.gpsimd.iota(first_i[:], [[P, TW]], base=0, channel_multiplier=0)
            nc.gpsimd.iota(my_first_i[:], [[P * P, TB]], base=0, channel_multiplier=P).then_inc(iotas_made, 1)

            pool.wait_ge(edges_stored, 16)
            pool.wait_ge(lo_ready, 1)
            for tb in range(TB):
                for w in range(WIN):
                    pool.indirect_dma_start(
                        out=window[:, tb, w], out_offset=None, in_=edge_table,
                        in_offset=bass.IndirectOffsetOnAxis(ap=lo_i[:, w, tb:tb + 1], axis=0),
                        bounds_check=KP - 1, oob_is_err=False).then_inc(window_loaded, 16)

            def step(ins):
                ins.then_inc(pool_step, 1)
                pool.wait_ge(pool_step, 1)
                pool.sem_clear(pool_step)

            G = nc.gpsimd

            def ln_coefs(s, h, base):
                q = base + s * 2 + h
                m_e, v_e, m_o, v_o = (stat6[:, h, :, i] for i in (1, 2, 4, 5))
                if not (base == 0 and isinstance(s, int) and s == 0):
                    pool.wait_ge(ln_applied, (q - 1) * GT)
                if base == 0:
                    pool.wait_ge(facts_copied, q + 1)
                pool.wait_ge(stats_ready, q + 1)
                G.tensor_tensor(ln_diff[:, h], m_e, m_o, ALU.subtract)
                G.tensor_tensor(ln_mean[:, h], m_e, m_o, ALU.add)
                step(G.tensor_tensor(ln_var[:, h], v_e, v_o, ALU.add))
                if base == 0:
                    nodes = ds(s * ST + h * GT, GT)
                    step(G.tensor_tensor(ln_base[:, h, 1], found[:, nodes, 0], counted[:, nodes, 0], ALU.add))
                    G.tensor_scalar(ln_base[:, h, 1], ln_base[:, h, 1], 1.0, None, ALU.add)
                G.tensor_scalar(ln_mean[:, h], ln_mean[:, h], -0.5, None, ALU.mult)
                G.tensor_scalar(ln_var[:, h], ln_var[:, h], 1.0 / D, EPS, ALU.mult, ALU.add)
                step(G.tensor_scalar(ln_diff[:, h], ln_diff[:, h], 0.5, None, ALU.mult))
                step(G.tensor_tensor(ln_diff[:, h], ln_diff[:, h], ln_diff[:, h], ALU.mult))
                step(G.tensor_tensor(ln_base[:, h, 0], ln_diff[:, h], ln_var[:, h], ALU.add))
                if base == 0:
                    step(G.tensor_tensor(ln_root[:, h], ln_base[:, h], power[:], ALU.pow))
                    G.tensor_copy(table[:, nodes, DIS], ln_root[:, h, 1]).then_inc(degrees_ready, 1)
                    step(G.tensor_tensor(ln_scale[:, h], ln_root[:, h, 0], ln_root[:, h, 1], ALU.mult))
                else:
                    step(G.tensor_tensor(ln_scale[:, h], ln_base[:, h, 0], power[:, 0], ALU.pow))
                G.tensor_tensor(ln_shift[:, h], ln_mean[:, h], ln_scale[:, h], ALU.mult).then_inc(ln_ready, 1)

            pool.wait_ge(counts_final, 1)
            for s in super_groups_last(pool):
                for h in range(2):
                    ln_coefs(s, h, 0)

            pool.wait_ge(flag_ready, 1)
            is_general = pool.value_load(general_i[0:1, 0:1], min_val=0, max_val=1)
            pool.wait_ge(table_ready, 1)
            pool.wait_ge(buffers_clear, 1)

            def settle(semaphore):
                pool.wait_ge(semaphore, 16)
                pool.dma_reset(range(semaphore.num, semaphore.num + 1))
                pool.sem_clear(semaphore)

            def gather_slots(layer, rows):
                base = (layer - 1) * T
                for s in super_groups(pool):
                    for h in range(2):
                        wait_free(pool, gather_issued, base + (s * 2 + h - 1) * GT)
                        if not (isinstance(s, int) and s == 0):
                            pool.wait_ge(agg_done, base + (s * 2 + h - 1) * GT)
                        nc.gpsimd.tensor_copy(idx_now[:, h], src_row[:, ds(s * ST + h * GT, GT)]).then_inc(idx_copied, 1)
                        pool.wait_ge(idx_copied, 1)
                        pool.sem_clear(idx_copied)
                        for g in range(GT):
                            j = h * GT + g
                            pool.indirect_dma_start(
                                out=neigh[:, j], out_offset=None, in_=rows,
                                in_offset=bass.IndirectOffsetOnAxis(ap=idx_now[:, h, g:g + 1], axis=0),
                                bounds_check=NP - 1, oob_is_err=False, engine_sem=gather_issued).then_inc(gathered[j], 16)
                        if layer == 2 and not (isinstance(s, int) and s == 0):
                            ln_coefs(s - 1, h, NQ)
                if layer == 2:
                    for h in range(2):
                        ln_coefs(NS - 1, h, NQ)

            for layer in range(1, 5):
                base = (layer - 1) * T
                rows = node_rows[layer - 1]
                for h in range(2):
                    if layer in (1, 3):
                        pool.wait_ge(normed_stored[h], 16 * NS * (1 if layer == 1 else 2))
                    else:
                        pool.wait_ge(rows_stored[h], 16 * NS * (layer - 1))
                with pool.If(is_general):
                    with pool.Fori(0, T) as t:
                        with pool.Fori(0, K) as k:
                            nc.gpsimd.tensor_copy(slow_idx[:], all_src_i[:, ds(k, 1)]).then_inc(slow_pool, 1)
                            pool.wait_ge(slow_pool, 1)
                            pool.sem_clear(slow_pool)
                            pool.indirect_dma_start(
                                out=neigh[:, 0], out_offset=None, in_=rows,
                                in_offset=bass.IndirectOffsetOnAxis(ap=slow_idx[:], axis=0),
                                bounds_check=NP - 1, oob_is_err=False).then_inc(slow_gathered, 16)
                            settle(slow_gathered)
                            pool.sem_inc(slow_rows_ready, 1)
                            pool.wait_ge(slow_next, 1)
                            pool.sem_clear(slow_next)
                        pool.wait_ge(slow_sum_ready, 1)
                        pool.sem_clear(slow_sum_ready)
                        pool.dma_start(sum_rows[ds(t * P, P), :], done_rows[:, 0, 0]).then_inc(slow_stored, 16)
                        settle(slow_stored)
                        pool.sem_inc(slow_sum_free, 1)
                    gather_slots(layer, sum_rows)
                with pool.Else():
                    gather_slots(layer, rows)

        @block.vector
        def _(dve):
            n_links = [0]

            def link(ins):
                n_links[0] += 1
                ins.then_inc(prep_dve, 1)
                dve.wait_ge(prep_dve, n_links[0])

            V = nc.vector

            def handshake(semaphore):
                dve.wait_ge(semaphore, 1)
                dve.sem_clear(semaphore)

            def general_counts():
                for i in range(3 * KB):
                    a, b = i // KB, i % KB
                    dve.wait_ge(slow_turned, i + 1)
                    V.tensor_copy([all_src, all_dst, all_self][a][:, b * P:(b + 1) * P],
                                  ps_prep[i % 2][:, 0:P]).then_inc(slow_turn_copied, 1)
                dve.wait_ge(slow_turn_copied, 3 * KB)
                V.scalar_tensor_tensor(out=all_dst_ns[:], in0=all_dst[:], scalar=1.0, in1=all_self[:],
                                       op0=ALU.add, op1=ALU.mult).then_inc(slow_dve, 1)
                handshake(slow_dve)
                V.tensor_scalar(all_dst_ns[:], all_dst_ns[:], 1.0, None, ALU.subtract)
                V.tensor_scalar(all_self[:], all_self[:], -1.0, 1.0, ALU.mult, ALU.add).then_inc(slow_dve, 1)
                handshake(slow_dve)
                V.scalar_tensor_tensor(out=all_src_i[:], in0=all_self[:], scalar=FAR, in1=all_src[:],
                                       op0=ALU.mult, op1=ALU.add)
                V.memset(slow_rhs[:, 0:1], 1.0).then_inc(slow_dve, 1)
                handshake(slow_dve)
                with dve.Fori(0, T) as t:
                    V.tensor_copy(slow_first[:], first_node[:, ds(t, 1)])
                    V.memset(counted_now[:], 0.0).then_inc(slow_dve, 1)
                    handshake(slow_dve)
                    with dve.Fori(0, K) as k:
                        V.tensor_copy(slow_rhs[:, 1:2], all_self[:, ds(k, 1)])
                        V.tensor_scalar(pick[:, 0], iota[:], slow_first[:, 0:1], all_dst[:, ds(k, 1)],
                                        ALU.add, ALU.is_equal).then_inc(slow_mm_wanted, 1)
                        handshake(slow_mm_done)
                        V.tensor_tensor(counted_now[:], counted_now[:], ps_prep[0][:, 0:2], ALU.add).then_inc(slow_dve, 1)
                        handshake(slow_dve)
                    V.tensor_copy(counted[:, ds(t, 1), :], counted_now[:].unsqueeze(1)).then_inc(slow_dve, 1)
                    handshake(slow_dve)

            def general_sums(layer):
                total = done_rows[:, 0, 0]
                for h in range(2):
                    if layer > 1:
                        dve.wait_ge(rows_stored[h], 16 * NS * (layer - 1))
                with dve.Fori(0, T) as t:
                    V.tensor_copy(slow_first[:], first_node[:, ds(t, 1)])
                    V.memset(total, 0.0).then_inc(slow_dve, 1)
                    handshake(slow_dve)
                    with dve.Fori(0, K) as k:
                        handshake(slow_rows_ready)
                        V.tensor_scalar(pick[:, 0], iota[:], slow_first[:, 0:1], all_dst_ns[:, ds(k, 1)],
                                        ALU.add, ALU.is_equal).then_inc(slow_mm_wanted, 1)
                        handshake(slow_mm_done)
                        V.tensor_tensor(total, total, ps_agg[0][:, 0:D], ALU.add).then_inc(slow_dve, 1)
                        handshake(slow_dve)
                        dve.sem_inc(slow_next, 1)
                    dve.sem_inc(slow_sum_ready, 1)
                    handshake(slow_sum_free)

            V.memset(src_i, PAD)
            V.memset(dst_i, PAD)
            link(V.memset(prev_i, PAD))
            V.memset(prev_i[0:1, 0, 0:1], -1).then_inc(pads_set, 1)
            V.memset(ones[:], 1.0)
            V.memset(counted[:], 0.0)
            V.memset(power[:], -0.5)
            V.memset(neigh[:], 0.0).then_inc(buffers_clear, 1)
            dve.wait_ge(iotas_made, 1)
            V.tensor_copy(iota[:], iota_i[:])
            V.tensor_copy(iota16[:], iota_i[:])
            V.tensor_copy(part[:], part_i[:])
            V.tensor_copy(first_node[:], first_i[:])
            link(V.tensor_copy(my_first[:], my_first_i[:]))
            V.tensor_scalar(my_first[:], my_first[:], float((T - 1) * P), None, ALU.min)
            V.tensor_scalar(ident[:], iota[:], part[:, 0:1], None, ALU.is_equal)
            V.tensor_scalar(before[:], iota[:], part[:, 0:1], None, ALU.is_gt)

            dve.wait_ge(edges_loaded, 16 * len(edge_pieces))
            V.tensor_copy(edges[:, :, 0], src_i)
            link(V.tensor_copy(edges[:, :, 1], dst_i))
            link(V.tensor_tensor(notself[:], edges[:, :, 0], edges[:, :, 1], ALU.not_equal))
            for b in range(KB):
                ins = V.tensor_tensor_scan(rank[:, b], ones[:], notself[:, b], 0.0, ALU.mult, ALU.add)
            link(ins)
            link(V.tensor_copy(totals[:, 0], rank[:, :, P - 1]))
            V.tensor_copy(work, prev_i).then_inc(counts_ready, 1)
            V.tensor_copy(small[:, 0], edges[:, :, 1, 0])
            V.tensor_copy(small[:, 1], edges[:, :, 1, P - 1])
            dve.wait_ge(counts_ready, 1)
            link(V.tensor_tensor(lead, edges[:, :, 1], work, ALU.subtract))
            V.tensor_reduce(bad[:, 0:1], lead, AX.XY, ALU.min)
            link(V.tensor_scalar(src_i, dst_i, 7, None, ALU.arith_shift_right))
            link(V.tensor_copy(tile_of, src_i))
            link(V.tensor_scalar(src_i, prev_i, 7, None, ALU.arith_shift_right))
            link(V.tensor_copy(work, src_i))
            link(V.tensor_tensor(lead, tile_of, work, ALU.not_equal))
            dve.wait_ge(bases_ready, 1)
            V.tensor_copy(totals[:, 1], ps_prep[0][:, 0:KB])
            link(V.tensor_copy(totals[:, 2], ps_prep[0][:, KB:2 * KB]))
            link(V.tensor_tensor_scan(totals[:, 3], ones[:, 0:KB], totals[:, 2], 0.0, ALU.mult, ALU.add))
            link(V.tensor_tensor(totals[:, 3], totals[:, 3], totals[:, 2], ALU.subtract))
            link(V.tensor_tensor(totals[:, 1], totals[:, 1], totals[:, 3], ALU.add))
            for b in range(KB):
                ins = V.scalar_tensor_tensor(out=rank[:, b], in0=rank[:, b], scalar=totals[:, 1, b:b + 1], in1=notself[:, b],
                                             op0=ALU.add, op1=ALU.subtract)
            link(ins)
            link(V.tensor_tensor(work, lead, rank, ALU.mult))
            for b in range(KB):
                ins = V.tensor_tensor_scan(lead[:, b], work[:, b], work[:, b], 0.0, ALU.max, ALU.max)
            link(ins)
            V.tensor_copy(small[:, 2], lead[:, :, P - 1]).then_inc(small_ready, 1)
            V.memset(carried[:, 0:1], 0.0)
            dve.wait_ge(rows_loaded, 16)
            link(V.tensor_tensor_scan(carried[:, 1:KP + 1], chunk_row[:, 2], chunk_row[:, 2], 0.0, ALU.max, ALU.max))
            link(V.tensor_tensor(work, carried[:, 0:KP].rearrange("p (b e) -> p b e", b=KB),
                                 ident[:].unsqueeze(1).to_broadcast([P, KB, P]), ALU.mult))
            link(V.tensor_reduce(totals[:, 0], work, AX.X, ALU.add))
            for b in range(KB):
                ins = V.scalar_tensor_tensor(out=work[:, b], in0=lead[:, b], scalar=totals[:, 0, b:b + 1], in1=rank[:, b],
                                             op0=ALU.max, op1=ALU.subtract)
            link(ins)
            link(V.scalar_tensor_tensor(out=lead, in0=tile_of, scalar=float(P), in1=work,
                                        op0=ALU.mult, op1=ALU.subtract))
            link(V.scalar_tensor_tensor(out=lead, in0=lead, scalar=1.0, in1=notself[:], op0=ALU.add, op1=ALU.mult))
            V.tensor_scalar(edges[:, :, 2], lead, 1.0, None, ALU.subtract).then_inc(edges_ready, 1)
            link(V.tensor_tensor(rank, work, notself[:], ALU.mult))
            V.tensor_reduce(bad[:, 1:2], rank, AX.XY, ALU.min)
            for tb in range(TB):
                link(V.tensor_scalar(work.rearrange("p b e -> p (b e)"), chunk_row[:, 1], my_first[:, tb:tb + 1], 0.0,
                                     ALU.is_lt, ALU.add, accum_out=lo[:, 0, tb:tb + 1]))
            link(V.tensor_scalar(lo[:, 2], my_first[:], float(P), None, ALU.add))
            for tb in range(TB):
                link(V.tensor_scalar(work.rearrange("p b e -> p (b e)"), chunk_row[:, 0], lo[:, 2, tb:tb + 1], 0.0,
                                     ALU.is_lt, ALU.add, accum_out=lo[:, 1, tb:tb + 1]))
            link(V.tensor_tensor(lo[:, 1], lo[:, 1], lo[:, 0], ALU.subtract))
            V.tensor_reduce(bad[:, 2:3], lo[:, 1], AX.X, ALU.max)
            link(V.tensor_scalar(lo[:, 0], lo[:, 0], float(KP - WIN), None, ALU.min))
            for w in range(WIN):
                ins = V.tensor_scalar(lo_i[:, w], lo[:, 0], float(w), None, ALU.add)
            ins.then_inc(lo_ready, 1)
            link(V.tensor_scalar(bad[:, 0:1], bad[:, 0:1], 0.0, None, ALU.is_lt))
            link(V.tensor_scalar(bad[:, 1:2], bad[:, 1:2], float(1 - P), None, ALU.is_lt))
            link(V.tensor_scalar(bad[:, 2:3], bad[:, 2:3], float(WIN), None, ALU.is_gt))
            V.tensor_reduce(bad[:, 3:4], bad[:, 0:3], AX.X, ALU.add).then_inc(bad_ready, 1)
            dve.wait_ge(bad_summed, 1)
            link(V.tensor_scalar(general[:, 0:1], ps_prep[1][:, 0:1], 0.0, None, ALU.is_gt))
            link(V.tensor_scalar(general[:, 1:2], general[:, 0:1], -1.0, 1.0, ALU.mult, ALU.add))
            V.tensor_copy(general_i[:], general[:, 0:1]).then_inc(flag_ready, 1)

            dve.wait_ge(window_loaded, 16 * TB * WIN)
            win = window.rearrange("p t w (c e) -> p t w c e", c=3)
            for tb in range(TB):
                V.tensor_tensor(own_loop[:, tb], win[:, tb, :, 0], win[:, tb, :, 1], ALU.is_equal)
            for tb in range(TB):
                for c in (1, 2):
                    ins = V.tensor_scalar(win[:, tb, :, c], win[:, tb, :, c], my_first[:, tb:tb + 1], None, ALU.subtract)
            ins.then_inc(window_ready, 1)
            for i in range(4 * WIN):
                a, w = i // WIN, i % WIN
                dve.wait_ge(win_turned, i + 1)
                V.tensor_copy(win_t[:, a, w], ps_prep[i % 2][:, 0:TW]).then_inc(win_copied, 1)
            dve.wait_ge(win_copied, 4 * WIN)
            link(V.tensor_copy(win_i, win_t[:, 2]))
            link(V.tensor_scalar(win_j, win_i, 8, None, ALU.arith_shift_right))
            link(V.tensor_copy(facts[:, :, :, 2], win_j))
            link(V.tensor_scalar(win_j, win_i, 255, None, ALU.bitwise_and))
            V.tensor_copy(facts[:, :, :, 3], win_j)
            V.memset(facts[:, :, :, 0], 1.0)
            V.tensor_copy(facts[:, :, :, 1], win_t[:, 3])
            link(V.tensor_scalar(facts[:, :, :, 4], win_t[:, 0], 1.0, None, ALU.add))

            dve.wait_ge(flag_ready, 1)
            is_general = dve.value_load(general_i[0:1, 0:1], min_val=0, max_val=1)
            with dve.If(is_general):
                general_counts()
            dve.sem_inc(counts_final, 1)

            def ln_stats(rows, s, h, base):
                if not (base == 0 and isinstance(s, int) and s == 0):
                    dve.wait_ge(ln_ready, base + s * 2 + h - 1)
                for g in range(GT):
                    ins = V.bn_stats(stat6[:, h, g], rows[:, h, g])
                ins.then_inc(stats_ready, 1)

            for s in super_groups_last(dve):
                for h in range(2):
                    wait_free(dve, facts_summed, (s * 2 + h - 1) * GT)
                    V.tensor_copy(key_now[:, h], win_t[:, 0:2, :, ds(s * ST + h * GT, GT)].rearrange(
                        "p a w g -> p (a w) g"))
                    V.tensor_copy(facts_now[:, h], facts[:, :, ds(s * ST + h * GT, GT), :]).then_inc(hits_ready, 1)
                    dve.wait_ge(hits_ready, (s * 2 + h) * (GT + 1) + 1)
                    for g in range(GT):
                        wait_free(dve, facts_summed, s * ST + h * GT + g - 3)
                        V.tensor_tensor(hits[:, g], iota16[:].unsqueeze(1).to_broadcast([P, 2 * WIN, P]),
                                        key_now[:, h, :, g:g + 1].to_broadcast([P, 2 * WIN, P]),
                                        ALU.is_equal).then_inc(hits_ready, 1)
                    dve.wait_ge(own_loaded[h], own_count(0, s, h))
                    ln_stats(own, s, h, 0)

            dve.wait_ge(facts_copied, NQ)
            dve.wait_ge(degrees_ready, NQ)

            table_f = [table[:, :, f] for f in range(NF)]
            link(V.tensor_tensor(found[:, :, 0:2], found[:, :, 0:2], counted[:], ALU.add))
            link(V.tensor_scalar(tmp_a[:], found[:, :, 0], 1.0, None, ALU.add))
            link(V.reciprocal(table_f[DIS2], tmp_a[:]))
            link(V.tensor_scalar(tmp_c[:], found[:, :, 0], 1.0, None, ALU.max))
            link(V.reciprocal(table_f[INV], tmp_c[:]))
            V.tensor_tensor(table_f[SELF_S], found[:, :, 1], table_f[INV], ALU.mult)
            link(V.scalar_tensor_tensor(out=table_f[SELF_G], in0=found[:, :, 1], scalar=1.0, in1=table_f[DIS2],
                                        op0=ALU.add, op1=ALU.mult))
            link(V.tensor_tensor(table_f[SQ], table_f[DIS], tmp_a[:], ALU.mult))
            link(V.tensor_scalar(tmp_a[:], found[:, :, 4], 1.0, None, ALU.subtract))
            link(V.tensor_scalar(tmp_a[:], tmp_a[:], general[:, 1:2], None, ALU.mult))
            link(V.tensor_scalar(tmp_b[:], general[:, 0:1].to_broadcast([P, T]), part[:, 0:1], None, ALU.mult))
            link(V.tensor_tensor(table_f[SLOT], tmp_a[:], tmp_b[:], ALU.add))
            V.tensor_scalar(tmp_c[:], found[:, :, 4], 0.5, FAR, ALU.is_lt, ALU.mult)
            link(V.scalar_tensor_tensor(out=tmp_a[:], in0=found[:, :, 2], scalar=256.0, in1=found[:, :, 3],
                                        op0=ALU.mult, op1=ALU.add))
            link(V.tensor_tensor(tmp_a[:], tmp_a[:], tmp_c[:], ALU.add))
            link(V.tensor_scalar(tmp_a[:], tmp_a[:], general[:, 1:2], None, ALU.mult))
            link(V.tensor_scalar(tmp_c[:], first_node[:, 0:T], part[:, 0:1], None, ALU.add))
            link(V.scalar_tensor_tensor(out=tmp_a[:], in0=tmp_c[:], scalar=general[:, 0:1], in1=tmp_a[:],
                                        op0=ALU.mult, op1=ALU.add))
            V.memset(table_f[NF - 1], 0.0)
            V.tensor_copy(src_row[:], tmp_a[:]).then_inc(table_ready, 1)
            dve.wait_ge(table_ready, 1)
            dve.wait_ge(weights_loaded, 16 * 12)
            for i in range(2):
                ins = V.tensor_tensor(bias[:, i], bias[:, i], res_bias[:], ALU.add)
            link(ins)

            for layer in range(1, 5):
                gcn = layer <= 2
                base = (layer - 1) * T
                gbase = (layer - 1) * NQ
                with dve.If(is_general):
                    general_sums(layer)
                K_PICK, K_SUM, K_OUT = 6, 4, 2

                def finish_pair(s, j):
                    h = j // GT
                    pair = ps_out[(j // 2) % 2]
                    q = s * 2 + h
                    if j % GT == 1:
                        wait_free(dve, rows_stored[h], ((layer - 1) * NS + s) * 16)
                        if layer == 2 and not (isinstance(s, int) and s == 0):
                            dve.wait_ge(ln_applied, (NQ + q - 1) * GT)
                        if layer == 4:
                            dve.wait_ge(resid_loaded[h], resid_count(4, s, h))
                    g = j % GT
                    dve.wait_ge(product_done, base + s * ST + j + 1)
                    if gcn:
                        for e in (0, 1):
                            o, p_ = done_rows[:, h, g - 1 + e], pair[:, e * D:(e + 1) * D]
                            if layer == 1:
                                ins = V.scalar_tensor_tensor(out=o, in0=bias[:, 0], scalar=scal[:, h, g - 1 + e, DIS:DIS + 1],
                                                             in1=p_, op0=ALU.mult, op1=ALU.add)
                            else:
                                ins = V.scalar_tensor_tensor(out=o, in0=p_, scalar=scal[:, h, g - 1 + e, SQ:SQ + 1],
                                                             in1=bias[:, 1], op0=ALU.mult, op1=ALU.add)
                    else:
                        o = done_rows[:, h, g - 1:g + 1]
                        p_ = pair[:].rearrange("p (a d) -> p a d", a=2)
                        other = (bias[:, 2].unsqueeze(1).to_broadcast([P, 2, D]) if layer == 3
                                 else resid[:, h, g - 1:g + 1])
                        ins = V.tensor_tensor(o, p_, other, ALU.add)
                    ins.then_inc(out_read, 1)
                    if g == GT - 1:
                        dve.wait_ge(out_read, base // 2 + s * (ST // 2) + (j + 1) // 2)
                        rows = done_rows[:, h].rearrange("p j d -> p (j d)")
                        if layer in (1, 3):
                            V.tensor_scalar(rows, rows, 0.0, None, ALU.max).then_inc(out_ready, 1)
                        elif layer == 2:
                            dve.wait_ge(resid_loaded[h], resid_count(2, s, h))
                            V.scalar_tensor_tensor(out=rows, in0=rows, scalar=0.0,
                                                   in1=resid[:, h].rearrange("p j d -> p (j d)"),
                                                   op0=ALU.max, op1=ALU.add).then_inc(out_ready, 1)
                            dve.wait_ge(out_ready, gbase + q + 1)
                            ln_stats(done_rows, s, h, NQ)
                        else:
                            V.tensor_tensor(done_rows[:, h], done_rows[:, h],
                                            bias[:, 3].unsqueeze(1).to_broadcast([P, GT, D]), ALU.add).then_inc(out_ready, 1)

                for s, j in tile_steps(dve, K_PICK, layer == 1):
                    c = at(s, j, K_PICK)
                    if c:
                        s_, j_ = c
                        h = j_ // GT
                        if j_ % GT == 0:
                            V.tensor_copy(scal[:, h], table[:, ds(s_ * ST + h * GT, GT), :]).then_inc(scal_ready, 1)
                            dve.wait_ge(scal_ready, gbase + s_ * 2 + h + 1)
                        wait_free(dve, agg_done, base + s_ * ST + j_ - 3)
                        V.tensor_scalar(pick[:, j_ % 4], iota[:], scal[:, h, j_ % GT, SLOT:SLOT + 1], None,
                                        ALU.is_equal).then_inc(pick_ready, 1)
                    c = at(s, j, K_SUM)
                    if c:
                        s_, j_ = c
                        n = base + s_ * ST + j_
                        f = DIS2 if gcn else INV
                        dve.wait_ge(agg_done, n + 1)
                        dve.wait_ge(self_ready, n + 1)
                        wait_free(dve, turn_done, n - 1)
                        V.scalar_tensor_tensor(out=agg[:, j_ % 2], in0=ps_agg[j_ % 2][:, 0:D],
                                               scalar=scal[:, j_ // GT, j_ % GT, f:f + 1], in1=selfpart[:, j_ % 4],
                                               op0=ALU.mult, op1=ALU.add).then_inc(combined, 1)
                    c = at(s, j, K_OUT)
                    if c and c[1] % 2 == 1:
                        finish_pair(*c)

        @block.scalar
        def _(act):
            def normalize(rows, base, s, h, tiles):
                for g in tiles:
                    nc.scalar.activation(normed[:, h, g], rows[:, h, g], ACT.Relu, scale=ln_scale[:, h, g:g + 1],
                                         bias=ln_shift[:, h, g:g + 1]).then_inc(ln_applied, 1)

            def store_normed(rows, base, s, h):
                act.wait_ge(ln_applied, (base + s * 2 + h + 1) * GT)
                act.dma_start(group_of(rows, s, h), normed[:, h]).then_inc(normed_stored[h], 16)

            def phase0_norm(s, h):
                act.wait_ge(ln_ready, s * 2 + h + 1)
                wait_free(act, normed_stored[h], s * 16)
                normalize(own, 0, s, h, range(GT))
                store_normed(node_rows[0], 0, s, h)

            act.wait_ge(flag_ready, 1)
            for s in super_groups_last(act):
                for h in range(2):
                    act.wait_ge(facts_summed, (s * 2 + h + 1) * GT)
                    nc.scalar.activation(found[:, ds(s * ST + h * GT, GT), :],
                                         ps_prep[h][:, 0:GT * 5].rearrange("p (g f) -> p g f", f=5), ACT.Copy,
                                         scale=general[:, 1:2]).then_inc(facts_copied, 1)
                    if h == 1:
                        phase0_norm(s, 0)
                    elif not (isinstance(s, int) and s == 0):
                        phase0_norm(s - 1, 1)
            phase0_norm(NS - 1, 1)

            for layer in range(1, 5):
                gcn = layer <= 2
                base = (layer - 1) * T
                gbase = (layer - 1) * NQ
                K_SELF, K_TURNED = (8, 6) if layer == 2 else (5, 3)
                K_STORE = 3 if layer == 2 else 0
                f = SELF_G if gcn else SELF_S

                for s, j in tile_steps(act, K_SELF, layer == 1):
                    c = at(s, j, K_SELF)
                    if c:
                        s_, j_ = c
                        h, n = j_ // GT, base + s_ * ST + j_
                        if j_ % GT == 0:
                            act.wait_ge(own_loaded[h], own_count(layer, s_, h))
                            act.wait_ge(scal_ready, gbase + s_ * 2 + h + 1)
                        wait_free(act, combined, n - 3)
                        nc.scalar.activation(selfpart[:, j_ % 4], own[:, h, j_ % GT], ACT.Copy,
                                             scale=scal[:, h, j_ % GT, f:f + 1]).then_inc(self_ready, 1)
                    c = at(s, j, K_TURNED)
                    if c:
                        s_, j_ = c
                        n = base + s_ * ST + j_
                        act.wait_ge(turn_done, n + 1)
                        wait_free(act, product_done, n - 1)
                        nc.scalar.copy(turned[:, j_ % 2], ps_turn[j_ % 2][:]).then_inc(turned_ready, 1)
                    c = at(s, j, K_STORE)
                    if c and c[1] % GT == GT - 1:
                        s_, h = c[0], c[1] // GT
                        act.wait_ge(out_ready, gbase + s_ * 2 + h + 1)
                        if layer < 4:
                            rows = x2_rows if layer == 2 else node_rows[layer]
                            act.dma_start(group_of(rows, s_, h), done_rows[:, h]).then_inc(rows_stored[h], 16)
                        elif isinstance(s_, int) and s_ == NS - 1:
                            for rows, (t0, t1), parts in short_group(out, h):
                                act.dma_start(rows, done_rows[0:parts, h, t0:t1]).then_inc(rows_stored[h], 16)
                        else:
                            act.dma_start(group_of(out, s_, h), done_rows[:, h]).then_inc(rows_stored[h], 16)
                    if layer == 2:
                        for k, half in ((2, (0, 1)), (1, (2, 3))):
                            c = at(s, j, k)
                            if c and c[1] % GT == GT - 1:
                                s_, h = c[0], c[1] // GT
                                if k == 2:
                                    act.wait_ge(ln_ready, NQ + s_ * 2 + h + 1)
                                    act.wait_ge(normed_stored[h], (NS + s_) * 16)
                                normalize(done_rows, NQ, s_, h, half)
                        c = at(s, j, 0)
                        if c and c[1] % GT == GT - 1:
                            store_normed(node_rows[2], NQ, c[0], c[1] // GT)
            for h in range(2):
                act.wait_ge(rows_stored[h], 16 * (4 * NS + last_dmas(h) - 1))
                act.wait_ge(normed_stored[h], 16 * 2 * NS)

        @block.tensor
        def _(pe):
            mm = nc.tensor.matmul
            pe.wait_ge(counts_ready, 1)
            mm(ps_prep[0][:, 0:KB], before[:], totals[:, 0], start=True, stop=True)
            mm(ps_prep[0][:, KB:2 * KB], ones[:], totals[:, 0], start=True, stop=True).then_inc(bases_ready, 1)
            pe.wait_ge(bad_ready, 1)
            mm(ps_prep[1][:, 0:1], ones[:], bad[:, 3:4], start=True, stop=True).then_inc(bad_summed, 1)
            pe.wait_ge(window_ready, 1)
            win = window.rearrange("p t w (c e) -> p t w c e", c=3)
            for i in range(4 * WIN):
                a, w = i // WIN, i % WIN
                if i >= 2:
                    pe.wait_ge(win_copied, i - 1)
                for tb in range(TB):
                    source = own_loop[:, tb, w] if a == 3 else win[:, tb, w, (1, 2, 0)[a]]
                    ins = nc.tensor.transpose(ps_prep[i % 2][:, tb * P:(tb + 1) * P], source, ident[:])
                ins.then_inc(win_turned, 1)
            pe.wait_ge(win_copied, 4 * WIN)
            pe.wait_ge(flag_ready, 1)
            is_general = pe.value_load(general_i[0:1, 0:1], min_val=0, max_val=1)
            with pe.If(is_general):
                for i in range(3 * KB):
                    a, b = i // KB, i % KB
                    if i >= 2:
                        pe.wait_ge(slow_turn_copied, i - 1)
                    source = notself[:, b] if a == 2 else edges[:, b, a]
                    nc.tensor.transpose(ps_prep[i % 2][:, 0:P], source, ident[:]).then_inc(slow_turned, 1)
                with pe.Fori(0, T) as t:
                    with pe.Fori(0, K) as k:
                        pe.wait_ge(slow_mm_wanted, 1)
                        pe.sem_clear(slow_mm_wanted)
                        mm(ps_prep[0][:, 0:2], pick[:, 0], slow_rhs[:], start=True, stop=True).then_inc(slow_mm_done, 1)

            for s in super_groups(pe):
                for h in range(2):
                    q = s * 2 + h
                    wait_free(pe, facts_copied, q - 1)
                    for g in range(GT):
                        pe.wait_ge(hits_ready, q * (GT + 1) + g + 2)
                        for a, (f0, f1) in enumerate(((0, 2), (2, 5))):
                            for w in range(WIN):
                                ins = mm(ps_prep[h][:, g * 5 + f0:g * 5 + f1], hits[:, g, a * WIN + w],
                                         facts_now[:, h, w, g, f0:f1], start=(w == 0), stop=(w == WIN - 1))
                        ins.then_inc(facts_summed, 1)

            pe.wait_ge(weights_loaded, 16 * 12)
            pe.wait_ge(buffers_clear, 1)
            for layer in range(1, 5):
                base = (layer - 1) * T
                w_sum, w_own = ((0, 2), (1, 2), (3, 4), (5, 6))[layer - 1]
                with pe.If(is_general):
                    with pe.Fori(0, T) as t:
                        with pe.Fori(0, K) as k:
                            pe.wait_ge(slow_mm_wanted, 1)
                            pe.sem_clear(slow_mm_wanted)
                            mm(ps_agg[0][:, 0:D], pick[:, 0], neigh[:, 0], start=True, stop=True).then_inc(slow_mm_done, 1)
                for s, j in tile_steps(pe, 4, layer == 1):
                    c = at(s, j, 4)
                    if c:
                        s_, j_ = c
                        n = base + s_ * ST + j_
                        pe.wait_ge(pick_ready, n + 1)
                        pe.wait_ge(gathered[j_], 16 * ((layer - 1) * NS + 1 + s_))
                        wait_free(pe, combined, n - 1)
                        mm(ps_agg[j_ % 2][:, 0:D], pick[:, j_ % 4], neigh[:, j_], start=True, stop=True).then_inc(agg_done, 1)
                    c = at(s, j, 3)
                    if c:
                        s_, j_ = c
                        h, n = j_ // GT, base + s_ * ST + j_
                        if j_ % GT == 0:
                            pe.wait_ge(own_loaded[h], own_count(layer, s_, h))
                        pe.wait_ge(combined, n + 1)
                        wait_free(pe, turned_ready, n - 1)
                        for b in range(2 * DC):
                            source = agg[:, j_ % 2] if b < DC else own[:, h, j_ % GT]
                            ins = nc.tensor.transpose(ps_turn[j_ % 2][:, b * P:(b + 1) * P],
                                                      source[:, (b % DC) * P:(b % DC + 1) * P], ident[:])
                        ins.then_inc(turn_done, 1)
                    c = at(s, j, 2)
                    if c:
                        s_, j_ = c
                        n = base + s_ * ST + j_
                        pe.wait_ge(turned_ready, n + 1)
                        if j_ % 2 == 0:
                            wait_free(pe, out_read, base // 2 + s_ * (ST // 2) + (j_ // 2 - 1))
                        o = ps_out[(j_ // 2) % 2][:, (j_ % 2) * D:(j_ % 2 + 1) * D]
                        for b in range(2 * DC):
                            ins = mm(o, turned[:, j_ % 2, b * P:(b + 1) * P], weights[:, (w_sum, w_own)[b // DC], b % DC],
                                     start=(b == 0), stop=(b == 2 * DC - 1))
                        ins.then_inc(product_done, 1)


_INS = ["x", "src", "dst", "L0_gnn_W", "L0_gnn_b", "L0_gnn_resW", "L0_gnn_resb", "L1_gnn_W1_l", "L1_gnn_W1_r",
        "L1_gnn_b1", "L1_gnn_W2_l", "L1_gnn_W2_r", "L1_gnn_b2"]


def kernel(**inputs):
    import numpy as _np
    import concourse.bacc as _bacc
    from concourse import mybir as _mybir
    from concourse.bass_utils import run_bass_kernel_spmd as _run

    nc = _bacc.Bacc("TRN2", target_bir_lowering=False, num_devices=1)
    arrays, args = {}, []
    for name in _INS:
        a = _np.ascontiguousarray(inputs[name])
        arrays[f"in_{name}_dram"] = a
        args.append(nc.dram_tensor(f"in_{name}_dram", a.shape, _mybir.dt.from_np(a.dtype), kind="ExternalInput").ap())
    shape = tuple(inputs["x"].shape)
    out = nc.dram_tensor("out_0_dram", shape, _mybir.dt.float32, kind="ExternalOutput").ap()
    gnn_kernel(nc, *args, out)
    r = _run(nc, [arrays], core_ids=[0])
    return r.results[0]["out_0_dram"]
```

```python
from contextlib import ExitStack

import concourse.bass as bass
from concourse import mybir

P = 128
D = 256
DC = D // P
GT = 4
ST = 8
WIN = 3
EPS = 1e-5
NF = 8
SLOT, SELF_G, DIS2, SELF_S, INV, DIS, SQ = range(7)
FAR = 1048576.0

F32 = mybir.dt.float32
F32R = mybir.dt.float32r
I32 = mybir.dt.int32
BF16 = mybir.dt.bfloat16
ALU = mybir.AluOpType
ACT = mybir.ActivationFunctionType
AX = mybir.AxisListType
ds = bass.ds


def ceil_div(a, b):
    return -(-a // b)


def gnn_kernel(nc, x, src, dst, gcn_w, gcn_b, res_w, res_b, sage1_l, sage1_r, sage1_b, sage2_l, sage2_r, sage2_b, out):
    N = x.shape[0]
    E = src.shape[0]
    NS = ceil_div(N, ST * P)
    T = NS * ST
    NQ = NS * 2
    NP = T * P
    K = ceil_div(E, P)
    KB = ceil_div(K + WIN, P)
    KP = KB * P
    PAD = T * P
    TB = ceil_div(T, P)
    TW = TB * P
    assert x.shape[1] == D and NS >= 4 and N > (NS - 1) * ST * P

    node_rows = [nc.dram_tensor(f"node_rows_{i}", [NP, D], F32).ap() for i in range(4)]
    sum_rows = nc.dram_tensor("sum_rows", [NP, D], F32).ap()
    x2_rows = nc.dram_tensor("x2_rows", [NP, D], F32).ap()
    edge_table = nc.dram_tensor("edge_table", [KP, 3 * P], F32).ap()
    chunk_rows = nc.dram_tensor("chunk_rows", [3, KP], F32).ap()

    with ExitStack() as ctx:
        def sb(name, shape, dt=F32):
            return ctx.enter_context(nc.sbuf_tensor(name, shape, dt))

        def psum(name):
            return ctx.enter_context(nc.psum_tensor(name, [P, 512], F32))

        def sem(name):
            return ctx.enter_context(nc.semaphore(name))

        own = sb("own", [P, 2, GT, D])
        assert TB * WIN * 4 * P <= 6 * GT * D
        shared = sb("shared", [P, 6 * GT * D])
        resid, done_rows, normed = (
            shared[:, i * 2 * GT * D:(i + 1) * 2 * GT * D].rearrange("p (h j d) -> p h j d", h=2, j=GT) for i in range(3))
        window = shared[:, 0:TB * WIN * 3 * P].rearrange("p (t w f) -> p t w f", t=TB, w=WIN)
        own_loop = shared[:, TB * WIN * 3 * P:TB * WIN * 4 * P].rearrange("p (t w e) -> p t w e", t=TB, w=WIN)
        neigh = sb("neigh", [P, ST, D])
        selfpart = sb("selfpart", [P, 4, D])
        agg = sb("agg", [P, 2, D])
        turned_hi = sb("turned_hi", [P, 2, 2 * D], F32R)
        turned_lo = sb("turned_lo", [P, 2, 2 * D], F32R)
        pick = sb("pick", [P, 4, P])
        scal = sb("scal", [P, 2, GT, NF])
        idx_now = sb("idx_now", [P, 2, GT], I32)
        assert 7 * DC * D <= 4 * GT * D
        weights = shared[:, 0:7 * DC * D].rearrange("p (i c d) -> p i c d", i=7, c=DC)
        weights_hi = sb("weights_hi", [P, 7, DC, D], F32R)
        weights_lo = sb("weights_lo", [P, 7, DC, D], F32R)
        bias = sb("bias", [P, 4, D])
        res_bias = sb("res_bias", [P, D])
        stat6 = sb("stat6", [P, 2, GT, 6])
        ln_mean = sb("ln_mean", [P, 2, GT])
        ln_diff = sb("ln_diff", [P, 2, GT])
        ln_var = sb("ln_var", [P, 2, GT])
        ln_base = sb("ln_base", [P, 2, 2, GT])
        ln_root = sb("ln_root", [P, 2, 2, GT])
        power = sb("power", [P, 2, GT])
        ln_scale = sb("ln_scale", [P, 2, GT])
        ln_shift = sb("ln_shift", [P, 2, GT])
        table = sb("table", [P, T, NF])
        src_row = sb("src_row", [P, T], I32)

        iota_i = sb("iota_i", [P, P], I32)
        part_i = sb("part_i", [P, 1], I32)
        first_i = sb("first_i", [P, TW], I32)
        iota = sb("iota", [P, P])
        iota16 = sb("iota16", [P, P], BF16)
        part = sb("part", [P, 1])
        first_node = sb("first_node", [P, TW])
        my_first = sb("my_first", [P, TB])
        my_first_i = sb("my_first_i", [P, TB], I32)
        ident = sb("ident", [P, P])
        before = sb("before", [P, P])
        ones = sb("ones", [P, P])

        assert 2 * WIN * TW <= 7 * KP
        edge_scratch = sb("edge_scratch", [P, 7 * KP], I32)

        def scratch(i, dt):
            part_of = edge_scratch[:, i * KP:(i + 1) * KP]
            return (part_of if dt == I32 else part_of.bitcast(dt)).rearrange("p (b e) -> p b e", b=KB)

        dst_i = scratch(0, I32)
        src_i = scratch(1, I32)
        prev_i = scratch(2, I32)
        edges = sb("edges", [P, KB, 3, P])
        tile_of = scratch(3, F32)
        notself = sb("notself", [P, KB, P])
        work = scratch(4, F32)
        rank = scratch(5, F32)
        lead = scratch(6, F32)
        small = sb("small", [P, 3, KB])
        totals = sb("totals", [P, 4, KB])
        chunk_row = sb("chunk_row", [P, 3, KP])
        carried = sb("carried", [P, KP + 1])
        lo = sb("lo", [P, 3, TB])
        lo_i = sb("lo_i", [P, WIN, TB], I32)
        win_t = sb("win_t", [P, 4, WIN, TW])
        win_i, win_j = (edge_scratch[:, i * WIN * TW:(i + 1) * WIN * TW].rearrange("p (w t) -> p w t", w=WIN)
                        for i in range(2))
        facts = sb("facts", [P, WIN, TW, 5], BF16)
        key_now = sb("key_now", [P, 2, 2 * WIN, GT], BF16)
        facts_now = sb("facts_now", [P, 2, WIN, GT, 5], BF16)
        hits = sb("hits", [P, 4, 2 * WIN, P], BF16)
        found = sb("found", [P, T, 5])
        counted = sb("counted", [P, T, 2])
        bad = sb("bad", [P, 4])
        general = sb("general", [P, 2])
        general_i = sb("general_i", [P, 1], I32)
        assert 5 * KP + 3 * T <= 7 * KP
        late_scratch = edge_scratch[:].bitcast(F32)
        tmp_a, tmp_b, tmp_c = (late_scratch[:, 5 * KP + i * T:5 * KP + (i + 1) * T] for i in range(3))
        all_src, all_dst, all_dst_ns, all_self = (late_scratch[:, i * KP:(i + 1) * KP] for i in range(4))
        all_src_i = edge_scratch[:, 4 * KP:5 * KP]
        slow_first = sb("slow_first", [P, 1])
        slow_idx = sb("slow_idx", [P, 1], I32)
        slow_rhs = sb("slow_rhs", [P, 2])
        counted_now = sb("counted_now", [P, 2])

        ps_agg = [psum("ps_agg0"), psum("ps_agg1")]
        ps_turn = [psum("ps_turn0"), psum("ps_turn1")]
        ps_out = [psum("ps_out0"), psum("ps_out1")]
        ps_prep = [psum("ps_prep0"), psum("ps_prep1")]

        iotas_made = sem("iotas_made")
        pads_set = sem("pads_set")
        edges_loaded = sem("edges_loaded")
        weights_loaded = sem("weights_loaded")
        prep_dve = sem("prep_dve")
        counts_ready = sem("counts_ready")
        bases_ready = sem("bases_ready")
        small_ready = sem("small_ready")
        rows_written = sem("rows_written")
        rows_loaded = sem("rows_loaded")
        edges_ready = sem("edges_ready")
        edges_stored = sem("edges_stored")
        lo_ready = sem("lo_ready")
        window_loaded = sem("window_loaded")
        window_ready = sem("window_ready")
        win_turned = sem("win_turned")
        win_copied = sem("win_copied")
        bad_ready = sem("bad_ready")
        bad_summed = sem("bad_summed")
        flag_ready = sem("flag_ready")
        hits_ready = sem("hits_ready")
        facts_summed = sem("facts_summed")
        facts_copied = sem("facts_copied")
        counts_final = sem("counts_final")
        degrees_ready = sem("degrees_ready")
        table_ready = sem("table_ready")
        slow_mm_wanted = sem("slow_mm_wanted")
        slow_mm_done = sem("slow_mm_done")
        slow_dve = sem("slow_dve")
        slow_pool = sem("slow_pool")
        slow_gathered = sem("slow_gathered")
        slow_rows_ready = sem("slow_rows_ready")
        slow_next = sem("slow_next")
        slow_sum_ready = sem("slow_sum_ready")
        slow_stored = sem("slow_stored")
        slow_sum_free = sem("slow_sum_free")
        slow_turned = sem("slow_turned")
        slow_turn_copied = sem("slow_turn_copied")
        x_loaded = [sem(f"x_loaded{i}") for i in range(4)]
        own_loaded = [sem("own_loaded0"), sem("own_loaded1")]
        resid_loaded = [sem("resid_loaded0"), sem("resid_loaded1")]
        rows_stored = [sem("rows_stored0"), sem("rows_stored1")]
        normed_stored = [sem("normed_stored0"), sem("normed_stored1")]
        gathered = [sem(f"gathered{j}") for j in range(ST)]
        gather_issued = sem("gather_issued")
        idx_copied = sem("idx_copied")
        scal_ready = sem("scal_ready")
        pick_ready = sem("pick_ready")
        self_ready = sem("self_ready")
        agg_done = sem("agg_done")
        combined = sem("combined")
        turn_done = sem("turn_done")
        turned_ready = sem("turned_ready")
        low_ready = sem("low_ready")
        weights_split = sem("weights_split")
        product_done = sem("product_done")
        out_read = sem("out_read")
        bias_added = sem("bias_added")
        relu_done = sem("relu_done")
        out_ready = sem("out_ready")
        stats_ready = sem("stats_ready")
        pool_step = sem("pool_step")
        ln_ready = sem("ln_ready")
        ln_applied = sem("ln_applied")

        def last_rows(h):
            return min(max(N - (NS - 1) * ST * P - h * GT * P, 0), GT * P)

        def last_dmas(h):
            r = last_rows(h)
            return (r >= P) + (r % P > 0)

        def group_of(rows, s, h):
            return rows[ds(s * (ST * P) + h * GT * P, GT * P), :].rearrange("(j p) d -> p j d", p=P)

        def short_group(rows, h):
            at, r = ((NS - 1) * ST + h * GT) * P, last_rows(h)
            full, rest = r // P, r % P
            pieces = []
            if full:
                pieces.append((rows[at:at + full * P, :].rearrange("(j p) d -> p j d", p=P), (0, full), P))
            if rest:
                pieces.append((rows[at + full * P:at + r, :].rearrange("(j p) d -> p j d", j=1), (full, full + 1), rest))
            return pieces

        def own_count(layer, s, h):
            return (layer - 1) * NS * 16 + (s + 1) * 16

        def x_buffer(slot):
            return own[:, slot] if slot < 2 else neigh[:, (slot - 2) * GT:(slot - 1) * GT]

        def x_count(s, turn, h):
            n = (turn + 1) * 16
            if isinstance(s, int) and s == NS - 1:
                n = n + (last_dmas(h) - 1) * 16
            return n

        def phase0_steps(eng):
            turns = (NS - 3) // 2
            yield 0, 0, 0
            yield 1, 0, 2
            if turns:
                with eng.Fori(1, 1 + turns) as turn:
                    yield turn * 2, turn, 0
                    yield turn * 2 + 1, turn, 2
            for s in range(2 + 2 * turns, NS):
                yield s, s // 2, s % 2 * 2

        def resid_count(layer, s, h):
            n = (NS if layer == 4 else 0) * 16 + (s + 1) * 16
            if layer == 4 or (isinstance(s, int) and s == NS - 1):
                n = n + (last_dmas(h) - 1) * 16
            return n

        def pairs_done(layer, s, j):
            return (layer - 1) * (T // 2) + s * (ST // 2) + (j + 1) // 2

        def super_groups(eng):
            yield 0
            with eng.Fori(1, NS) as s:
                yield s

        def super_groups_last(eng):
            yield 0
            with eng.Fori(1, NS - 1) as s:
                yield s
            yield NS - 1

        def tile_steps(eng, ahead, first):
            for j in range(-ahead, ST if first else 0):
                yield 0, j
            with eng.Fori(1 if first else 0, NS - 1) as s:
                for j in range(ST):
                    yield s, j
            for j in range(ST):
                yield NS - 1, j

        def at(s, j, k):
            if j + k < 0 or (isinstance(s, int) and s == NS - 1 and j + k >= ST):
                return None
            i = j + k
            return s + i // ST, i % ST

        def wait_free(eng, semaphore, value):
            if not (isinstance(value, int) and value <= 0):
                eng.wait_ge(semaphore, value)

        edge_pieces = []
        for pair, shift in (((src_i, src), 0), ((dst_i, dst), 0), ((prev_i, dst), 1)):
            for b in range(KB):
                first, row = b * P * P - shift, 0
                if first < 0:
                    edge_pieces.append((pair, (0, 1), 0, 0, P - shift, shift))
                    first, row = P - shift, 1
                full = min(P - row, max(E - first, 0) // P)
                if full:
                    edge_pieces.append((pair, (row, row + full), first, b, P, 0))
                rest = min(E - first - full * P, P)
                if row + full < P and rest > 0:
                    edge_pieces.append((pair, (row + full, row + full + 1), first + full * P, b, rest, 0))

        block = ctx.enter_context(nc.Block())

        @block.sync
        def _(sp):
            sp.wait_ge(pads_set, 1)
            for flat, rows, first, b, width, skip in edge_pieces:
                n = width if rows[1] - rows[0] == 1 else P
                count = (rows[1] - rows[0] - 1) * P + n
                sp.dma_start(flat[0][rows[0]:rows[1], b, skip:skip + n],
                             flat[1][first:first + count].rearrange("(p e) -> p e", e=n)).then_inc(edges_loaded, 16)
            sp.wait_ge(small_ready, 1)
            with nc.allow_non_contiguous_dma("a few values for each chunk"):
                sp.dma_start(chunk_rows.rearrange("c (b p) -> p c b", p=P), small[:]).then_inc(rows_written, 16)
            sp.wait_ge(rows_written, 16)
            sp.dma_start(chunk_row[:].rearrange("p c k -> p (c k)"),
                         chunk_rows.rearrange("c k -> (c k)").partition_broadcast(P)).then_inc(rows_loaded, 16)
            sp.wait_ge(edges_ready, 1)
            sp.dma_start(edge_table.rearrange("(b p) f -> p b f", p=P),
                         edges[:].rearrange("p b c e -> p b (c e)")).then_inc(edges_stored, 16)

            for s, turn, slot in phase0_steps(sp):
                for h in range(2):
                    wait_free(sp, ln_applied, (s * 2 + h - 3) * GT)
                    rows_now = x_buffer(slot + h)
                    if isinstance(s, int) and s == NS - 1:
                        for rows, (t0, t1), parts in short_group(x, h):
                            sp.dma_start(rows_now[0:parts, t0:t1], rows).then_inc(x_loaded[slot + h], 16)
                    else:
                        sp.dma_start(rows_now, group_of(x, s, h)).then_inc(x_loaded[slot + h], 16)
                if isinstance(s, int) and s == 1:
                    sp.wait_ge(win_turned, 4 * WIN)
                    mats = [gcn_w[0], gcn_w[1], res_w, sage1_l, sage1_r, sage2_l, sage2_r]
                    for i, m in enumerate(mats):
                        sp.dma_start(weights[:, i], m.rearrange("(c p) n -> p c n", p=P)).then_inc(weights_loaded, 16)
                    biases = [gcn_b[0], gcn_b[1], sage1_b, sage2_b]
                    for i, v in enumerate(biases):
                        sp.dma_start(bias[:, i], v.partition_broadcast(P)).then_inc(weights_loaded, 16)
                    sp.dma_start(res_bias[:], res_b.partition_broadcast(P)).then_inc(weights_loaded, 16)

            for layer in range(1, 5):
                base = (layer - 1) * T
                if layer in (1, 3):
                    for h in range(2):
                        sp.wait_ge(normed_stored[h], 16 * NS * (1 if layer == 1 else 2))
                else:
                    for h in range(2):
                        sp.wait_ge(rows_stored[h], 16 * NS * (layer - 1))
                for s in super_groups_last(sp):
                    for h in range(2):
                        if not (isinstance(s, int) and s == 0):
                            sp.wait_ge(turn_done, base + (s * 2 + h - 1) * GT)
                            sp.wait_ge(self_ready, base + (s * 2 + h - 1) * GT)
                        sp.dma_start(own[:, h], group_of(node_rows[layer - 1], s, h)).then_inc(own_loaded[h], 16)
                        if layer in (2, 4):
                            if not (isinstance(s, int) and s == 0):
                                if layer == 2:
                                    sp.wait_ge(out_ready, (s * 2 + h - 1) * (GT // 2))
                                else:
                                    sp.wait_ge(out_read, 3 * (T // 2) + (s * 2 + h - 1) * (GT // 2))
                            if layer == 4:
                                sp.dma_start(resid[:, h], group_of(x2_rows, s, h)).then_inc(resid_loaded[h], 16)
                            elif isinstance(s, int) and s == NS - 1:
                                for rows, (t0, t1), parts in short_group(x, h):
                                    sp.dma_start(resid[0:parts, h, t0:t1], rows).then_inc(resid_loaded[h], 16)
                            else:
                                sp.dma_start(resid[:, h], group_of(x, s, h)).then_inc(resid_loaded[h], 16)

        @block.gpsimd
        def _(pool):
            nc.gpsimd.iota(iota_i[:], [[1, P]], base=0, channel_multiplier=0)
            nc.gpsimd.iota(part_i[:], [[0, 1]], base=0, channel_multiplier=1)
            nc.gpsimd.iota(first_i[:], [[P, TW]], base=0, channel_multiplier=0)
            nc.gpsimd.iota(my_first_i[:], [[P * P, TB]], base=0, channel_multiplier=P).then_inc(iotas_made, 1)

            pool.wait_ge(edges_stored, 16)
            pool.wait_ge(lo_ready, 1)
            for tb in range(TB):
                for w in range(WIN):
                    pool.indirect_dma_start(
                        out=window[:, tb, w], out_offset=None, in_=edge_table,
                        in_offset=bass.IndirectOffsetOnAxis(ap=lo_i[:, w, tb:tb + 1], axis=0),
                        bounds_check=KP - 1, oob_is_err=False).then_inc(window_loaded, 16)

            def step(ins):
                ins.then_inc(pool_step, 1)
                pool.wait_ge(pool_step, 1)
                pool.sem_clear(pool_step)

            G = nc.gpsimd

            def ln_coefs(s, h, base):
                q = base + s * 2 + h
                m_e, v_e, m_o, v_o = (stat6[:, h, :, i] for i in (1, 2, 4, 5))
                if not (base == 0 and isinstance(s, int) and s == 0):
                    pool.wait_ge(ln_applied, (q - 1) * GT)
                if base == 0:
                    pool.wait_ge(facts_copied, q + 1)
                pool.wait_ge(stats_ready, q + 1)
                G.tensor_tensor(ln_diff[:, h], m_e, m_o, ALU.subtract)
                G.tensor_tensor(ln_mean[:, h], m_e, m_o, ALU.add)
                step(G.tensor_tensor(ln_var[:, h], v_e, v_o, ALU.add))
                if base == 0:
                    nodes = ds(s * ST + h * GT, GT)
                    step(G.tensor_tensor(ln_base[:, h, 1], found[:, nodes, 0], counted[:, nodes, 0], ALU.add))
                    G.tensor_scalar(ln_base[:, h, 1], ln_base[:, h, 1], 1.0, None, ALU.add)
                G.tensor_scalar(ln_mean[:, h], ln_mean[:, h], -0.5, None, ALU.mult)
                G.tensor_scalar(ln_var[:, h], ln_var[:, h], 1.0 / D, EPS, ALU.mult, ALU.add)
                step(G.tensor_scalar(ln_diff[:, h], ln_diff[:, h], 0.5, None, ALU.mult))
                step(G.tensor_tensor(ln_diff[:, h], ln_diff[:, h], ln_diff[:, h], ALU.mult))
                step(G.tensor_tensor(ln_base[:, h, 0], ln_diff[:, h], ln_var[:, h], ALU.add))
                if base == 0:
                    step(G.tensor_tensor(ln_root[:, h], ln_base[:, h], power[:], ALU.pow))
                    G.tensor_copy(table[:, nodes, DIS], ln_root[:, h, 1]).then_inc(degrees_ready, 1)
                    step(G.tensor_tensor(ln_scale[:, h], ln_root[:, h, 0], ln_root[:, h, 1], ALU.mult))
                else:
                    step(G.tensor_tensor(ln_scale[:, h], ln_base[:, h, 0], power[:, 0], ALU.pow))
                G.tensor_tensor(ln_shift[:, h], ln_mean[:, h], ln_scale[:, h], ALU.mult).then_inc(ln_ready, 1)

            pool.wait_ge(counts_final, 1)
            for s, turn, slot in phase0_steps(pool):
                for h in range(2):
                    ln_coefs(s, h, 0)

            pool.wait_ge(flag_ready, 1)
            is_general = pool.value_load(general_i[0:1, 0:1], min_val=0, max_val=1)
            pool.wait_ge(table_ready, 1)

            def settle(semaphore):
                pool.wait_ge(semaphore, 16)
                pool.dma_reset(range(semaphore.num, semaphore.num + 1))
                pool.sem_clear(semaphore)

            def add_bias(s, h):
                pool.wait_ge(resid_loaded[h], resid_count(4, s, h))
                G.tensor_tensor(resid[:, h], resid[:, h], bias[:, 3].unsqueeze(1).to_broadcast([P, GT, D]),
                                ALU.add).then_inc(bias_added, 1)

            def gather_slots(layer, rows):
                base = (layer - 1) * T
                for s in super_groups(pool):
                    for h in range(2):
                        wait_free(pool, gather_issued, base + (s * 2 + h - 1) * GT)
                        if not (isinstance(s, int) and s == 0):
                            pool.wait_ge(agg_done, base + (s * 2 + h - 1) * GT)
                        nc.gpsimd.tensor_copy(idx_now[:, h], src_row[:, ds(s * ST + h * GT, GT)]).then_inc(idx_copied, 1)
                        pool.wait_ge(idx_copied, 1)
                        pool.sem_clear(idx_copied)
                        for g in range(GT):
                            j = h * GT + g
                            pool.indirect_dma_start(
                                out=neigh[:, j], out_offset=None, in_=rows,
                                in_offset=bass.IndirectOffsetOnAxis(ap=idx_now[:, h, g:g + 1], axis=0),
                                bounds_check=NP - 1, oob_is_err=False, engine_sem=gather_issued).then_inc(gathered[j], 16)
                        if layer == 4:
                            if h == 1:
                                add_bias(s, 0)
                            elif not (isinstance(s, int) and s == 0):
                                add_bias(s - 1, 1)
                        if layer == 2 and not (isinstance(s, int) and s == 0):
                            ln_coefs(s - 1, h, NQ)
                if layer == 2:
                    for h in range(2):
                        ln_coefs(NS - 1, h, NQ)
                if layer == 4:
                    add_bias(NS - 1, 1)

            for layer in range(1, 5):
                base = (layer - 1) * T
                rows = node_rows[layer - 1]
                for h in range(2):
                    if layer in (1, 3):
                        pool.wait_ge(normed_stored[h], 16 * NS * (1 if layer == 1 else 2))
                    else:
                        pool.wait_ge(rows_stored[h], 16 * NS * (layer - 1))
                with pool.If(is_general):
                    with pool.Fori(0, T) as t:
                        with pool.Fori(0, K) as k:
                            nc.gpsimd.tensor_copy(slow_idx[:], all_src_i[:, ds(k, 1)]).then_inc(slow_pool, 1)
                            pool.wait_ge(slow_pool, 1)
                            pool.sem_clear(slow_pool)
                            pool.indirect_dma_start(
                                out=neigh[:, 0], out_offset=None, in_=rows,
                                in_offset=bass.IndirectOffsetOnAxis(ap=slow_idx[:], axis=0),
                                bounds_check=NP - 1, oob_is_err=False).then_inc(slow_gathered, 16)
                            settle(slow_gathered)
                            pool.sem_inc(slow_rows_ready, 1)
                            pool.wait_ge(slow_next, 1)
                            pool.sem_clear(slow_next)
                        pool.wait_ge(slow_sum_ready, 1)
                        pool.sem_clear(slow_sum_ready)
                        pool.dma_start(sum_rows[ds(t * P, P), :], done_rows[:, 0, 0]).then_inc(slow_stored, 16)
                        settle(slow_stored)
                        pool.sem_inc(slow_sum_free, 1)
                    gather_slots(layer, sum_rows)
                with pool.Else():
                    gather_slots(layer, rows)

        @block.vector
        def _(dve):
            n_links = [0]

            def link(ins):
                n_links[0] += 1
                ins.then_inc(prep_dve, 1)
                dve.wait_ge(prep_dve, n_links[0])

            V = nc.vector

            def handshake(semaphore):
                dve.wait_ge(semaphore, 1)
                dve.sem_clear(semaphore)

            def general_counts():
                for i in range(3 * KB):
                    a, b = i // KB, i % KB
                    dve.wait_ge(slow_turned, i + 1)
                    V.tensor_copy([all_src, all_dst, all_self][a][:, b * P:(b + 1) * P],
                                  ps_prep[i % 2][:, 0:P]).then_inc(slow_turn_copied, 1)
                dve.wait_ge(slow_turn_copied, 3 * KB)
                V.scalar_tensor_tensor(out=all_dst_ns, in0=all_dst, scalar=1.0, in1=all_self,
                                       op0=ALU.add, op1=ALU.mult).then_inc(slow_dve, 1)
                handshake(slow_dve)
                V.tensor_scalar(all_dst_ns, all_dst_ns, 1.0, None, ALU.subtract)
                V.tensor_scalar(all_self, all_self, -1.0, 1.0, ALU.mult, ALU.add).then_inc(slow_dve, 1)
                handshake(slow_dve)
                V.scalar_tensor_tensor(out=all_src_i, in0=all_self, scalar=FAR, in1=all_src,
                                       op0=ALU.mult, op1=ALU.add)
                V.memset(slow_rhs[:, 0:1], 1.0).then_inc(slow_dve, 1)
                handshake(slow_dve)
                with dve.Fori(0, T) as t:
                    V.tensor_copy(slow_first[:], first_node[:, ds(t, 1)])
                    V.memset(counted_now[:], 0.0).then_inc(slow_dve, 1)
                    handshake(slow_dve)
                    with dve.Fori(0, K) as k:
                        V.tensor_copy(slow_rhs[:, 1:2], all_self[:, ds(k, 1)])
                        V.tensor_scalar(pick[:, 0], iota[:], slow_first[:, 0:1], all_dst[:, ds(k, 1)],
                                        ALU.add, ALU.is_equal).then_inc(slow_mm_wanted, 1)
                        handshake(slow_mm_done)
                        V.tensor_tensor(counted_now[:], counted_now[:], ps_prep[0][:, 0:2], ALU.add).then_inc(slow_dve, 1)
                        handshake(slow_dve)
                    V.tensor_copy(counted[:, ds(t, 1), :], counted_now[:].unsqueeze(1)).then_inc(slow_dve, 1)
                    handshake(slow_dve)

            def general_sums(layer):
                total = done_rows[:, 0, 0]
                for h in range(2):
                    if layer > 1:
                        dve.wait_ge(rows_stored[h], 16 * NS * (layer - 1))
                with dve.Fori(0, T) as t:
                    V.tensor_copy(slow_first[:], first_node[:, ds(t, 1)])
                    V.memset(total, 0.0).then_inc(slow_dve, 1)
                    handshake(slow_dve)
                    with dve.Fori(0, K) as k:
                        handshake(slow_rows_ready)
                        V.tensor_scalar(pick[:, 0], iota[:], slow_first[:, 0:1], all_dst_ns[:, ds(k, 1)],
                                        ALU.add, ALU.is_equal).then_inc(slow_mm_wanted, 1)
                        handshake(slow_mm_done)
                        V.tensor_tensor(total, total, ps_agg[0][:, 0:D], ALU.add).then_inc(slow_dve, 1)
                        handshake(slow_dve)
                        dve.sem_inc(slow_next, 1)
                    dve.sem_inc(slow_sum_ready, 1)
                    handshake(slow_sum_free)

            V.memset(src_i, PAD)
            V.memset(dst_i, PAD)
            link(V.memset(prev_i, PAD))
            V.memset(prev_i[0:1, 0, 0:1], -1).then_inc(pads_set, 1)
            V.memset(ones[:], 1.0)
            V.memset(counted[:], 0.0)
            V.memset(power[:], -0.5)
            dve.wait_ge(iotas_made, 1)
            V.tensor_copy(iota[:], iota_i[:])
            V.tensor_copy(iota16[:], iota_i[:])
            V.tensor_copy(part[:], part_i[:])
            V.tensor_copy(first_node[:], first_i[:])
            link(V.tensor_copy(my_first[:], my_first_i[:]))
            V.tensor_scalar(my_first[:], my_first[:], float((T - 1) * P), None, ALU.min)
            V.tensor_scalar(ident[:], iota[:], part[:, 0:1], None, ALU.is_equal)
            V.tensor_scalar(before[:], iota[:], part[:, 0:1], None, ALU.is_gt)

            dve.wait_ge(edges_loaded, 16 * len(edge_pieces))
            V.tensor_copy(edges[:, :, 0], src_i)
            link(V.tensor_copy(edges[:, :, 1], dst_i))
            link(V.tensor_tensor(notself[:], edges[:, :, 0], edges[:, :, 1], ALU.not_equal))
            for b in range(KB):
                ins = V.tensor_tensor_scan(rank[:, b], ones[:], notself[:, b], 0.0, ALU.mult, ALU.add)
            link(ins)
            link(V.tensor_copy(totals[:, 0], rank[:, :, P - 1]))
            V.tensor_copy(work, prev_i).then_inc(counts_ready, 1)
            V.tensor_copy(small[:, 0], edges[:, :, 1, 0])
            V.tensor_copy(small[:, 1], edges[:, :, 1, P - 1])
            dve.wait_ge(counts_ready, 1)
            link(V.tensor_tensor(lead, edges[:, :, 1], work, ALU.subtract))
            V.tensor_reduce(bad[:, 0:1], lead, AX.XY, ALU.min)
            link(V.tensor_scalar(src_i, dst_i, 7, None, ALU.arith_shift_right))
            link(V.tensor_copy(tile_of, src_i))
            link(V.tensor_scalar(src_i, prev_i, 7, None, ALU.arith_shift_right))
            link(V.tensor_copy(work, src_i))
            link(V.tensor_tensor(lead, tile_of, work, ALU.not_equal))
            dve.wait_ge(bases_ready, 1)
            V.tensor_copy(totals[:, 1], ps_prep[0][:, 0:KB])
            link(V.tensor_copy(totals[:, 2], ps_prep[0][:, KB:2 * KB]))
            link(V.tensor_tensor_scan(totals[:, 3], ones[:, 0:KB], totals[:, 2], 0.0, ALU.mult, ALU.add))
            link(V.tensor_tensor(totals[:, 3], totals[:, 3], totals[:, 2], ALU.subtract))
            link(V.tensor_tensor(totals[:, 1], totals[:, 1], totals[:, 3], ALU.add))
            for b in range(KB):
                ins = V.scalar_tensor_tensor(out=rank[:, b], in0=rank[:, b], scalar=totals[:, 1, b:b + 1], in1=notself[:, b],
                                             op0=ALU.add, op1=ALU.subtract)
            link(ins)
            link(V.tensor_tensor(work, lead, rank, ALU.mult))
            for b in range(KB):
                ins = V.tensor_tensor_scan(lead[:, b], work[:, b], work[:, b], 0.0, ALU.max, ALU.max)
            link(ins)
            V.tensor_copy(small[:, 2], lead[:, :, P - 1]).then_inc(small_ready, 1)
            V.memset(carried[:, 0:1], 0.0)
            dve.wait_ge(rows_loaded, 16)
            link(V.tensor_tensor_scan(carried[:, 1:KP + 1], chunk_row[:, 2], chunk_row[:, 2], 0.0, ALU.max, ALU.max))
            link(V.tensor_tensor(work, carried[:, 0:KP].rearrange("p (b e) -> p b e", b=KB),
                                 ident[:].unsqueeze(1).to_broadcast([P, KB, P]), ALU.mult))
            link(V.tensor_reduce(totals[:, 0], work, AX.X, ALU.add))
            for b in range(KB):
                ins = V.scalar_tensor_tensor(out=work[:, b], in0=lead[:, b], scalar=totals[:, 0, b:b + 1], in1=rank[:, b],
                                             op0=ALU.max, op1=ALU.subtract)
            link(ins)
            link(V.scalar_tensor_tensor(out=lead, in0=tile_of, scalar=float(P), in1=work,
                                        op0=ALU.mult, op1=ALU.subtract))
            link(V.scalar_tensor_tensor(out=lead, in0=lead, scalar=1.0, in1=notself[:], op0=ALU.add, op1=ALU.mult))
            V.tensor_scalar(edges[:, :, 2], lead, 1.0, None, ALU.subtract).then_inc(edges_ready, 1)
            link(V.tensor_tensor(rank, work, notself[:], ALU.mult))
            V.tensor_reduce(bad[:, 1:2], rank, AX.XY, ALU.min)
            for tb in range(TB):
                link(V.tensor_scalar(work.rearrange("p b e -> p (b e)"), chunk_row[:, 1], my_first[:, tb:tb + 1], 0.0,
                                     ALU.is_lt, ALU.add, accum_out=lo[:, 0, tb:tb + 1]))
            link(V.tensor_scalar(lo[:, 2], my_first[:], float(P), None, ALU.add))
            for tb in range(TB):
                link(V.tensor_scalar(work.rearrange("p b e -> p (b e)"), chunk_row[:, 0], lo[:, 2, tb:tb + 1], 0.0,
                                     ALU.is_lt, ALU.add, accum_out=lo[:, 1, tb:tb + 1]))
            link(V.tensor_tensor(lo[:, 1], lo[:, 1], lo[:, 0], ALU.subtract))
            V.tensor_reduce(bad[:, 2:3], lo[:, 1], AX.X, ALU.max)
            link(V.tensor_scalar(lo[:, 0], lo[:, 0], float(KP - WIN), None, ALU.min))
            for w in range(WIN):
                ins = V.tensor_scalar(lo_i[:, w], lo[:, 0], float(w), None, ALU.add)
            ins.then_inc(lo_ready, 1)
            link(V.tensor_scalar(bad[:, 0:1], bad[:, 0:1], 0.0, None, ALU.is_lt))
            link(V.tensor_scalar(bad[:, 1:2], bad[:, 1:2], float(1 - P), None, ALU.is_lt))
            link(V.tensor_scalar(bad[:, 2:3], bad[:, 2:3], float(WIN), None, ALU.is_gt))
            V.tensor_reduce(bad[:, 3:4], bad[:, 0:3], AX.X, ALU.add).then_inc(bad_ready, 1)
            dve.wait_ge(bad_summed, 1)
            link(V.tensor_scalar(general[:, 0:1], ps_prep[1][:, 0:1], 0.0, None, ALU.is_gt))
            link(V.tensor_scalar(general[:, 1:2], general[:, 0:1], -1.0, 1.0, ALU.mult, ALU.add))
            V.tensor_copy(general_i[:], general[:, 0:1]).then_inc(flag_ready, 1)

            dve.wait_ge(window_loaded, 16 * TB * WIN)
            win = window.rearrange("p t w (c e) -> p t w c e", c=3)
            for tb in range(TB):
                V.tensor_tensor(own_loop[:, tb], win[:, tb, :, 0], win[:, tb, :, 1], ALU.is_equal)
            for tb in range(TB):
                for c in (1, 2):
                    ins = V.tensor_scalar(win[:, tb, :, c], win[:, tb, :, c], my_first[:, tb:tb + 1], None, ALU.subtract)
            ins.then_inc(window_ready, 1)
            for i in range(4 * WIN):
                a, w = i // WIN, i % WIN
                dve.wait_ge(win_turned, i + 1)
                V.tensor_copy(win_t[:, a, w], ps_prep[i % 2][:, 0:TW]).then_inc(win_copied, 1)
            dve.wait_ge(win_copied, 4 * WIN)
            link(V.tensor_copy(win_i, win_t[:, 2]))
            link(V.tensor_scalar(win_j, win_i, 8, None, ALU.arith_shift_right))
            link(V.tensor_copy(facts[:, :, :, 2], win_j))
            link(V.tensor_scalar(win_j, win_i, 255, None, ALU.bitwise_and))
            V.tensor_copy(facts[:, :, :, 3], win_j)
            V.memset(facts[:, :, :, 0], 1.0)
            V.tensor_copy(facts[:, :, :, 1], win_t[:, 3])
            link(V.tensor_scalar(facts[:, :, :, 4], win_t[:, 0], 1.0, None, ALU.add))

            dve.wait_ge(flag_ready, 1)
            is_general = dve.value_load(general_i[0:1, 0:1], min_val=0, max_val=1)
            with dve.If(is_general):
                general_counts()
            dve.sem_inc(counts_final, 1)

            for s, turn, slot in phase0_steps(dve):
                for h in range(2):
                    wait_free(dve, facts_summed, (s * 2 + h - 1) * GT)
                    V.tensor_copy(key_now[:, h], win_t[:, 0:2, :, ds(s * ST + h * GT, GT)].rearrange(
                        "p a w g -> p (a w) g"))
                    V.tensor_copy(facts_now[:, h], facts[:, :, ds(s * ST + h * GT, GT), :]).then_inc(hits_ready, 1)
                    dve.wait_ge(hits_ready, (s * 2 + h) * (GT + 1) + 1)
                    for g in range(GT):
                        wait_free(dve, facts_summed, s * ST + h * GT + g - 3)
                        V.tensor_tensor(hits[:, g], iota16[:].unsqueeze(1).to_broadcast([P, 2 * WIN, P]),
                                        key_now[:, h, :, g:g + 1].to_broadcast([P, 2 * WIN, P]),
                                        ALU.is_equal).then_inc(hits_ready, 1)
                    dve.wait_ge(x_loaded[slot + h], x_count(s, turn, h))
                    wait_free(dve, ln_ready, s * 2 + h - 1)
                    for g in range(GT):
                        ins = V.bn_stats(stat6[:, h, g], x_buffer(slot + h)[:, g])
                    ins.then_inc(stats_ready, 1)

            dve.wait_ge(facts_copied, NQ)
            dve.wait_ge(degrees_ready, NQ)

            table_f = [table[:, :, f] for f in range(NF)]
            link(V.tensor_tensor(found[:, :, 0:2], found[:, :, 0:2], counted[:], ALU.add))
            link(V.tensor_scalar(tmp_a, found[:, :, 0], 1.0, None, ALU.add))
            link(V.reciprocal(table_f[DIS2], tmp_a))
            link(V.tensor_scalar(tmp_c, found[:, :, 0], 1.0, None, ALU.max))
            link(V.reciprocal(table_f[INV], tmp_c))
            V.tensor_tensor(table_f[SELF_S], found[:, :, 1], table_f[INV], ALU.mult)
            link(V.scalar_tensor_tensor(out=table_f[SELF_G], in0=found[:, :, 1], scalar=1.0, in1=table_f[DIS2],
                                        op0=ALU.add, op1=ALU.mult))
            link(V.tensor_tensor(table_f[SQ], table_f[DIS], tmp_a, ALU.mult))
            link(V.tensor_scalar(tmp_a, found[:, :, 4], 1.0, None, ALU.subtract))
            link(V.tensor_scalar(tmp_a, tmp_a, general[:, 1:2], None, ALU.mult))
            link(V.tensor_scalar(tmp_b, general[:, 0:1].to_broadcast([P, T]), part[:, 0:1], None, ALU.mult))
            link(V.tensor_tensor(table_f[SLOT], tmp_a, tmp_b, ALU.add))
            V.tensor_scalar(tmp_c, found[:, :, 4], 0.5, FAR, ALU.is_lt, ALU.mult)
            link(V.scalar_tensor_tensor(out=tmp_a, in0=found[:, :, 2], scalar=256.0, in1=found[:, :, 3],
                                        op0=ALU.mult, op1=ALU.add))
            link(V.tensor_tensor(tmp_a, tmp_a, tmp_c, ALU.add))
            link(V.tensor_scalar(tmp_a, tmp_a, general[:, 1:2], None, ALU.mult))
            link(V.tensor_scalar(tmp_c, first_node[:, 0:T], part[:, 0:1], None, ALU.add))
            link(V.scalar_tensor_tensor(out=tmp_a, in0=tmp_c, scalar=general[:, 0:1], in1=tmp_a,
                                        op0=ALU.mult, op1=ALU.add))
            V.memset(table_f[NF - 1], 0.0)
            V.tensor_copy(src_row[:], tmp_a).then_inc(table_ready, 1)
            dve.wait_ge(table_ready, 1)
            dve.wait_ge(weights_loaded, 16 * 12)
            link(V.tensor_copy(weights_hi[:], weights))
            V.tensor_tensor(weights_lo[:], weights, weights_hi[:].bitcast(F32), ALU.subtract).then_inc(weights_split, 1)
            dve.wait_ge(weights_split, 1)
            for i in range(2):
                ins = V.tensor_tensor(bias[:, i], bias[:, i], res_bias[:], ALU.add)
            link(ins)

            for layer in range(1, 5):
                gcn = layer <= 2
                base = (layer - 1) * T
                gbase = (layer - 1) * NQ
                with dve.If(is_general):
                    general_sums(layer)
                K_PICK, K_SUM, K_LOW, K_OUT, K_RESID, K_STATS = 6, 5, 4, 2, 1, 0

                def finish_pair(s, j):
                    h, g = j // GT, j % GT
                    pair = ps_out[(j // 2) % 2]
                    if g == 1:
                        wait_free(dve, rows_stored[h], ((layer - 1) * NS + s) * 16)
                        if layer == 2 and not (isinstance(s, int) and s == 0):
                            dve.wait_ge(ln_applied, (NQ + s * 2 + h - 1) * GT)
                        if layer == 4:
                            dve.wait_ge(bias_added, s * 2 + h + 1)
                    dve.wait_ge(product_done, base + s * ST + j + 1)
                    if gcn:
                        for e in (0, 1):
                            o, p_ = done_rows[:, h, g - 1 + e], pair[:, e * D:(e + 1) * D]
                            if layer == 1:
                                ins = V.scalar_tensor_tensor(out=o, in0=bias[:, 0], scalar=scal[:, h, g - 1 + e, DIS:DIS + 1],
                                                             in1=p_, op0=ALU.mult, op1=ALU.add)
                            else:
                                ins = V.scalar_tensor_tensor(out=o, in0=p_, scalar=scal[:, h, g - 1 + e, SQ:SQ + 1],
                                                             in1=bias[:, 1], op0=ALU.mult, op1=ALU.add)
                    else:
                        o = done_rows[:, h, g - 1:g + 1]
                        p_ = pair[:].rearrange("p (a d) -> p a d", a=2)
                        other = (bias[:, 2].unsqueeze(1).to_broadcast([P, 2, D]) if layer == 3
                                 else resid[:, h, g - 1:g + 1])
                        ins = V.tensor_tensor(o, p_, other, ALU.add)
                    ins.then_inc(out_read, 1)

                def add_resid(s, j):
                    h, g = j // GT, j % GT
                    if g == 1:
                        dve.wait_ge(resid_loaded[h], resid_count(2, s, h))
                    dve.wait_ge(out_read, pairs_done(2, s, j))
                    rows = done_rows[:, h, g - 1:g + 1].rearrange("p j d -> p (j d)")
                    V.scalar_tensor_tensor(out=rows, in0=rows, scalar=0.0,
                                           in1=resid[:, h, g - 1:g + 1].rearrange("p j d -> p (j d)"),
                                           op0=ALU.max, op1=ALU.add).then_inc(out_ready, 1)

                def tile_stats(s, j):
                    h, g = j // GT, j % GT
                    if g == 0:
                        dve.wait_ge(ln_ready, NQ + s * 2 + h - 1)
                    dve.wait_ge(out_ready, pairs_done(1, s, j | 1))
                    ins = V.bn_stats(stat6[:, h, g], done_rows[:, h, g])
                    if g == GT - 1:
                        ins.then_inc(stats_ready, 1)

                for s, j in tile_steps(dve, K_PICK, layer == 1):
                    c = at(s, j, K_OUT)
                    if c and c[1] % 2 == 1:
                        finish_pair(*c)
                    c = at(s, j, K_PICK)
                    if c:
                        s_, j_ = c
                        h = j_ // GT
                        if j_ % GT == 0:
                            wait_free(dve, out_read, (layer - 1) * (T // 2) + (s_ * 2 + h - 1) * (GT // 2))
                            V.tensor_copy(scal[:, h], table[:, ds(s_ * ST + h * GT, GT), :]).then_inc(scal_ready, 1)
                            dve.wait_ge(scal_ready, gbase + s_ * 2 + h + 1)
                        wait_free(dve, agg_done, base + s_ * ST + j_ - 3)
                        V.tensor_scalar(pick[:, j_ % 4], iota[:], scal[:, h, j_ % GT, SLOT:SLOT + 1], None,
                                        ALU.is_equal).then_inc(pick_ready, 1)
                    c = at(s, j, K_SUM)
                    if c:
                        s_, j_ = c
                        n = base + s_ * ST + j_
                        f = DIS2 if gcn else INV
                        dve.wait_ge(agg_done, n + 1)
                        dve.wait_ge(self_ready, n + 1)
                        wait_free(dve, turn_done, n - 1)
                        V.scalar_tensor_tensor(out=agg[:, j_ % 2], in0=ps_agg[j_ % 2][:, 0:D],
                                               scalar=scal[:, j_ // GT, j_ % GT, f:f + 1], in1=selfpart[:, j_ % 4],
                                               op0=ALU.mult, op1=ALU.add).then_inc(combined, 1)
                    c = at(s, j, K_LOW)
                    if c:
                        s_, j_ = c
                        n = base + s_ * ST + j_
                        dve.wait_ge(turned_ready, n + 1)
                        wait_free(dve, product_done, n - 1)
                        V.tensor_tensor(turned_lo[:, j_ % 2], ps_turn[j_ % 2][:], turned_hi[:, j_ % 2].bitcast(F32),
                                        ALU.subtract).then_inc(low_ready, 1)
                    if layer == 2:
                        c = at(s, j, K_RESID)
                        if c and c[1] % 2 == 1:
                            add_resid(*c)
                        c = at(s, j, K_STATS)
                        if c:
                            tile_stats(*c)

        @block.scalar
        def _(act):
            def normalize(rows, h, tiles):
                for g in tiles:
                    nc.scalar.activation(normed[:, h, g], rows[:, g], ACT.Relu, scale=ln_scale[:, h, g:g + 1],
                                         bias=ln_shift[:, h, g:g + 1]).then_inc(ln_applied, 1)

            def store_normed(rows, base, s, h):
                act.wait_ge(ln_applied, (base + s * 2 + h + 1) * GT)
                act.dma_start(group_of(rows, s, h), normed[:, h]).then_inc(normed_stored[h], 16)

            def phase0_norm(s, h, slot):
                act.wait_ge(ln_ready, s * 2 + h + 1)
                wait_free(act, normed_stored[h], s * 16)
                normalize(x_buffer(slot), h, range(GT))
                store_normed(node_rows[0], 0, s, h)

            act.wait_ge(flag_ready, 1)
            for s, turn, slot in phase0_steps(act):
                for h in range(2):
                    act.wait_ge(facts_summed, (s * 2 + h + 1) * GT)
                    nc.scalar.activation(found[:, ds(s * ST + h * GT, GT), :],
                                         ps_prep[h][:, 0:GT * 5].rearrange("p (g f) -> p g f", f=5), ACT.Copy,
                                         scale=general[:, 1:2]).then_inc(facts_copied, 1)
                    if h == 1:
                        phase0_norm(s, 0, slot)
                    elif not (isinstance(s, int) and s == 0):
                        phase0_norm(s - 1, 1, 3 - slot)
            phase0_norm(NS - 1, 1, (NS - 1) % 2 * 2 + 1)

            for layer in range(1, 5):
                gcn = layer <= 2
                base = (layer - 1) * T
                gbase = (layer - 1) * NQ
                K_SELF, K_TURNED = (8, 7) if layer == 2 else (6, 4)
                K_STORE = 2 if layer == 2 else 0
                f = SELF_G if gcn else SELF_S

                for s, j in tile_steps(act, K_SELF, layer == 1):
                    c = at(s, j, K_SELF)
                    if c:
                        s_, j_ = c
                        h, n = j_ // GT, base + s_ * ST + j_
                        if j_ % GT == 0:
                            act.wait_ge(own_loaded[h], own_count(layer, s_, h))
                            act.wait_ge(scal_ready, gbase + s_ * 2 + h + 1)
                        wait_free(act, combined, n - 3)
                        nc.scalar.activation(selfpart[:, j_ % 4], own[:, h, j_ % GT], ACT.Copy,
                                             scale=scal[:, h, j_ % GT, f:f + 1]).then_inc(self_ready, 1)
                    c = at(s, j, K_TURNED)
                    if c:
                        s_, j_ = c
                        n = base + s_ * ST + j_
                        act.wait_ge(turn_done, n + 1)
                        wait_free(act, product_done, n - 1)
                        nc.scalar.copy(turned_hi[:, j_ % 2], ps_turn[j_ % 2][:]).then_inc(turned_ready, 1)
                    c = at(s, j, 1)
                    if layer in (1, 3) and c and c[1] % 2 == 1:
                        s_, h, g = c[0], c[1] // GT, c[1] % GT
                        act.wait_ge(out_read, pairs_done(layer, s_, c[1]))
                        nc.scalar.activation(done_rows[:, h, g - 1:g + 1], done_rows[:, h, g - 1:g + 1],
                                             ACT.Relu).then_inc(relu_done, 1)
                    c = at(s, j, K_STORE)
                    if c and c[1] % GT == GT - 1:
                        s_, h = c[0], c[1] // GT
                        if layer in (1, 3):
                            act.wait_ge(relu_done, pairs_done(1 if layer == 1 else 2, s_, c[1]))
                        elif layer == 2:
                            act.wait_ge(out_ready, pairs_done(1, s_, c[1]))
                        else:
                            act.wait_ge(out_read, pairs_done(layer, s_, c[1]))
                        if layer < 4:
                            rows = x2_rows if layer == 2 else node_rows[layer]
                            act.dma_start(group_of(rows, s_, h), done_rows[:, h]).then_inc(rows_stored[h], 16)
                        elif isinstance(s_, int) and s_ == NS - 1:
                            for rows, (t0, t1), parts in short_group(out, h):
                                act.dma_start(rows, done_rows[0:parts, h, t0:t1]).then_inc(rows_stored[h], 16)
                        else:
                            act.dma_start(group_of(out, s_, h), done_rows[:, h]).then_inc(rows_stored[h], 16)
                    if layer == 2:
                        for k, half in ((1, (0, 1)), (0, (2, 3))):
                            c = at(s, j, k)
                            if c and c[1] % GT == GT - 1:
                                s_, h = c[0], c[1] // GT
                                if k == 1:
                                    act.wait_ge(ln_ready, NQ + s_ * 2 + h + 1)
                                    act.wait_ge(normed_stored[h], (NS + s_) * 16)
                                normalize(done_rows[:, h], h, half)
                        c = at(s, j, 0)
                        if c and c[1] % GT == GT - 1:
                            store_normed(node_rows[2], NQ, c[0], c[1] // GT)
            for h in range(2):
                act.wait_ge(rows_stored[h], 16 * (4 * NS + last_dmas(h) - 1))
                act.wait_ge(normed_stored[h], 16 * 2 * NS)

        @block.tensor
        def _(pe):
            mm = nc.tensor.matmul
            pe.wait_ge(counts_ready, 1)
            mm(ps_prep[0][:, 0:KB], before[:], totals[:, 0], start=True, stop=True)
            mm(ps_prep[0][:, KB:2 * KB], ones[:], totals[:, 0], start=True, stop=True).then_inc(bases_ready, 1)
            pe.wait_ge(bad_ready, 1)
            mm(ps_prep[1][:, 0:1], ones[:], bad[:, 3:4], start=True, stop=True).then_inc(bad_summed, 1)
            pe.wait_ge(window_ready, 1)
            win = window.rearrange("p t w (c e) -> p t w c e", c=3)
            for i in range(4 * WIN):
                a, w = i // WIN, i % WIN
                if i >= 2:
                    pe.wait_ge(win_copied, i - 1)
                for tb in range(TB):
                    source = own_loop[:, tb, w] if a == 3 else win[:, tb, w, (1, 2, 0)[a]]
                    ins = nc.tensor.transpose(ps_prep[i % 2][:, tb * P:(tb + 1) * P], source, ident[:])
                ins.then_inc(win_turned, 1)
            pe.wait_ge(win_copied, 4 * WIN)
            pe.wait_ge(flag_ready, 1)
            is_general = pe.value_load(general_i[0:1, 0:1], min_val=0, max_val=1)
            with pe.If(is_general):
                for i in range(3 * KB):
                    a, b = i // KB, i % KB
                    if i >= 2:
                        pe.wait_ge(slow_turn_copied, i - 1)
                    source = notself[:, b] if a == 2 else edges[:, b, a]
                    nc.tensor.transpose(ps_prep[i % 2][:, 0:P], source, ident[:]).then_inc(slow_turned, 1)
                with pe.Fori(0, T) as t:
                    with pe.Fori(0, K) as k:
                        pe.wait_ge(slow_mm_wanted, 1)
                        pe.sem_clear(slow_mm_wanted)
                        mm(ps_prep[0][:, 0:2], pick[:, 0], slow_rhs[:], start=True, stop=True).then_inc(slow_mm_done, 1)

            for s in super_groups(pe):
                for h in range(2):
                    q = s * 2 + h
                    wait_free(pe, facts_copied, q - 1)
                    for g in range(GT):
                        pe.wait_ge(hits_ready, q * (GT + 1) + g + 2)
                        for a, (f0, f1) in enumerate(((0, 2), (2, 5))):
                            for w in range(WIN):
                                ins = mm(ps_prep[h][:, g * 5 + f0:g * 5 + f1], hits[:, g, a * WIN + w],
                                         facts_now[:, h, w, g, f0:f1], start=(w == 0), stop=(w == WIN - 1))
                        ins.then_inc(facts_summed, 1)

            pe.wait_ge(weights_split, 1)
            for layer in range(1, 5):
                base = (layer - 1) * T
                w_sum, w_own = ((0, 2), (1, 2), (3, 4), (5, 6))[layer - 1]
                with pe.If(is_general):
                    with pe.Fori(0, T) as t:
                        with pe.Fori(0, K) as k:
                            pe.wait_ge(slow_mm_wanted, 1)
                            pe.sem_clear(slow_mm_wanted)
                            mm(ps_agg[0][:, 0:D], pick[:, 0], neigh[:, 0], start=True, stop=True).then_inc(slow_mm_done, 1)
                for s, j in tile_steps(pe, 4, layer == 1):
                    c = at(s, j, 4)
                    if c:
                        s_, j_ = c
                        n = base + s_ * ST + j_
                        pe.wait_ge(pick_ready, n + 1)
                        pe.wait_ge(gathered[j_], 16 * ((layer - 1) * NS + 1 + s_))
                        wait_free(pe, combined, n - 1)
                        mm(ps_agg[j_ % 2][:, 0:D], pick[:, j_ % 4], neigh[:, j_], start=True, stop=True).then_inc(agg_done, 1)
                    c = at(s, j, 3)
                    if c:
                        s_, j_ = c
                        h, n = j_ // GT, base + s_ * ST + j_
                        if j_ % GT == 0:
                            pe.wait_ge(own_loaded[h], own_count(layer, s_, h))
                        pe.wait_ge(combined, n + 1)
                        wait_free(pe, low_ready, n - 1)
                        for b in range(2 * DC):
                            source = agg[:, j_ % 2] if b < DC else own[:, h, j_ % GT]
                            ins = nc.tensor.transpose(ps_turn[j_ % 2][:, b * P:(b + 1) * P],
                                                      source[:, (b % DC) * P:(b % DC + 1) * P], ident[:])
                        ins.then_inc(turn_done, 1)
                    c = at(s, j, 2)
                    if c:
                        s_, j_ = c
                        n = base + s_ * ST + j_
                        pe.wait_ge(low_ready, n + 1)
                        if j_ % 2 == 0:
                            wait_free(pe, out_read, base // 2 + s_ * (ST // 2) + (j_ // 2 - 1))
                        o = ps_out[(j_ // 2) % 2][:, (j_ % 2) * D:(j_ % 2 + 1) * D]
                        parts = ((turned_lo, weights_hi), (turned_hi, weights_lo), (turned_hi, weights_hi))
                        for b in range(2 * DC):
                            for i, (left, right) in enumerate(parts):
                                ins = mm(o, left[:, j_ % 2, b * P:(b + 1) * P], right[:, (w_sum, w_own)[b // DC], b % DC],
                                         start=(b + i == 0), stop=(b == 2 * DC - 1 and i == 2))
                        ins.then_inc(product_done, 1)


_INS = ["x", "src", "dst", "L0_gnn_W", "L0_gnn_b", "L0_gnn_resW", "L0_gnn_resb", "L1_gnn_W1_l", "L1_gnn_W1_r",
        "L1_gnn_b1", "L1_gnn_W2_l", "L1_gnn_W2_r", "L1_gnn_b2"]


def kernel(**inputs):
    import numpy as _np
    import concourse.bacc as _bacc
    from concourse import mybir as _mybir
    from concourse.bass_utils import run_bass_kernel_spmd as _run

    nc = _bacc.Bacc("TRN2", target_bir_lowering=False, num_devices=1)
    arrays, args = {}, []
    for name in _INS:
        a = _np.ascontiguousarray(inputs[name])
        arrays[f"in_{name}_dram"] = a
        args.append(nc.dram_tensor(f"in_{name}_dram", a.shape, _mybir.dt.from_np(a.dtype), kind="ExternalInput").ap())
    shape = tuple(inputs["x"].shape)
    out = nc.dram_tensor("out_0_dram", shape, _mybir.dt.float32, kind="ExternalOutput").ap()
    gnn_kernel(nc, *args, out)
    r = _run(nc, [arrays], core_ids=[0])
    return r.results[0]["out_0_dram"]
```

```python
from contextlib import ExitStack

import concourse.bass as bass
from concourse import mybir

P = 128
D = 256
DC = D // P
GT = 4
ST = 8
WIN = 3
EPS = 1e-5
NF = 8
SLOT, SELF_G, DIS2, SELF_S, INV, DIS, SQ = range(7)
FAR = 1048576.0

F32 = mybir.dt.float32
F32R = mybir.dt.float32r
I32 = mybir.dt.int32
BF16 = mybir.dt.bfloat16
ALU = mybir.AluOpType
ACT = mybir.ActivationFunctionType
AX = mybir.AxisListType
ds = bass.ds


def ceil_div(a, b):
    return -(-a // b)


def gnn_kernel(nc, x, src, dst, gcn_w, gcn_b, res_w, res_b, sage1_l, sage1_r, sage1_b, sage2_l, sage2_r, sage2_b, out):
    N = x.shape[0]
    E = src.shape[0]
    NS = ceil_div(N, ST * P)
    T = NS * ST
    NQ = NS * 2
    NP = T * P
    K = ceil_div(E, P)
    KB = ceil_div(K + WIN, P)
    KP = KB * P
    PAD = T * P
    TB = ceil_div(T, P)
    TW = TB * P
    assert x.shape[1] == D and NS >= 4 and N > (NS - 1) * ST * P

    node_rows = [nc.dram_tensor(f"node_rows_{i}", [NP, D], F32).ap() for i in range(4)]
    sum_rows = nc.dram_tensor("sum_rows", [NP, D], F32).ap()
    x2_rows = nc.dram_tensor("x2_rows", [NP, D], F32).ap()
    edge_table = nc.dram_tensor("edge_table", [KP, 3 * P], F32).ap()
    chunk_rows = nc.dram_tensor("chunk_rows", [3, KP], F32).ap()

    with ExitStack() as ctx:
        def sb(name, shape, dt=F32):
            return ctx.enter_context(nc.sbuf_tensor(name, shape, dt))

        def psum(name):
            return ctx.enter_context(nc.psum_tensor(name, [P, 512], F32))

        def sem(name):
            return ctx.enter_context(nc.semaphore(name))

        own = sb("own", [P, 2, GT, D])
        assert TB * WIN * 4 * P <= 6 * GT * D
        shared = sb("shared", [P, 6 * GT * D])
        resid, done_rows, normed = (
            shared[:, i * 2 * GT * D:(i + 1) * 2 * GT * D].rearrange("p (h j d) -> p h j d", h=2, j=GT) for i in range(3))
        window = shared[:, 0:TB * WIN * 3 * P].rearrange("p (t w f) -> p t w f", t=TB, w=WIN)
        own_loop = shared[:, TB * WIN * 3 * P:TB * WIN * 4 * P].rearrange("p (t w e) -> p t w e", t=TB, w=WIN)
        neigh = sb("neigh", [P, ST, D])
        turned_hi = sb("turned_hi", [P, 4, 2 * D], F32R)
        turned_lo = sb("turned_lo", [P, 4, 2 * D], F32R)
        pick = sb("pick", [P, 4, P])
        scal = sb("scal", [P, 2, GT, NF])
        idx_now = sb("idx_now", [P, 2, GT], I32)
        assert 7 * DC * D <= 4 * GT * D
        weights = shared[:, 0:7 * DC * D].rearrange("p (i c d) -> p i c d", i=7, c=DC)
        weights_hi = sb("weights_hi", [P, 7, DC, D], F32R)
        weights_lo = sb("weights_lo", [P, 7, DC, D], F32R)
        bias = sb("bias", [P, 4, D])
        res_bias = sb("res_bias", [P, D])
        stat6 = sb("stat6", [P, 4, GT, 6])
        ln_sum = sb("ln_sum", [P, 2, GT, 3])
        ln_factor = sb("ln_factor", [P, GT, 3])
        ln_base = sb("ln_base", [P, 2, 2, GT])
        ln_root = sb("ln_root", [P, 2, 2, GT])
        power = sb("power", [P, 2, GT])
        ln_scale = sb("ln_scale", [P, 2, GT])
        ln_shift = sb("ln_shift", [P, 2, GT])
        table = sb("table", [P, T, NF])
        src_row = sb("src_row", [P, T], I32)

        iota_i = sb("iota_i", [P, P], I32)
        part_i = sb("part_i", [P, 1], I32)
        first_i = sb("first_i", [P, TW], I32)
        iota = sb("iota", [P, P])
        iota16 = sb("iota16", [P, P], BF16)
        part = sb("part", [P, 1])
        first_node = sb("first_node", [P, TW])
        my_first = sb("my_first", [P, TB])
        my_first_i = sb("my_first_i", [P, TB], I32)
        ident = sb("ident", [P, P])
        before = sb("before", [P, P])
        ones = sb("ones", [P, P])

        assert 2 * WIN * TW <= 7 * KP
        edge_scratch = sb("edge_scratch", [P, 7 * KP], I32)

        def scratch(i, dt):
            part_of = edge_scratch[:, i * KP:(i + 1) * KP]
            return (part_of if dt == I32 else part_of.bitcast(dt)).rearrange("p (b e) -> p b e", b=KB)

        dst_i = scratch(0, I32)
        src_i = scratch(1, I32)
        prev_i = scratch(2, I32)
        edge_bytes = sb("edges", [P, max(KB * 3 * P, 2 * WIN * P)])
        edges = edge_bytes[:, 0:KB * 3 * P].rearrange("p (b c e) -> p b c e", b=KB, c=3)
        tile_of = scratch(3, F32)
        notself = sb("notself", [P, KB, P])
        work = scratch(4, F32)
        rank = scratch(5, F32)
        lead = scratch(6, F32)
        small = sb("small", [P, 3, KB])
        totals = sb("totals", [P, 4, KB])
        chunk_bytes = sb("chunk_row", [P, max(3 * KP, 6 * D)])
        chunk_row = chunk_bytes[:, 0:3 * KP].rearrange("p (c k) -> p c k", c=3)
        layer_scratch = chunk_bytes
        selfpart = layer_scratch[:, 0:4 * D].rearrange("p (j d) -> p j d", j=4)
        agg = layer_scratch[:, 4 * D:6 * D].rearrange("p (j d) -> p j d", j=2)
        carried = sb("carried", [P, KP + 1])
        lo = sb("lo", [P, 3, TB])
        lo_i = sb("lo_i", [P, WIN, TB], I32)
        win_t = sb("win_t", [P, 4, WIN, TW])
        win_i, win_j = (edge_scratch[:, i * WIN * TW:(i + 1) * WIN * TW].rearrange("p (w t) -> p w t", w=WIN)
                        for i in range(2))
        facts = sb("facts", [P, WIN, TW, 4], BF16)
        key_now = sb("key_now", [P, 2, WIN, GT], BF16)
        facts_now = sb("facts_now", [P, 2, WIN, GT, 4], BF16)
        ends = sb("ends", [P, 2, GT, P], BF16)
        one16 = sb("one16", [P, 1], BF16)
        iota16_1 = sb("iota16_1", [P, P], BF16)
        hits = edge_bytes[:, 0:2 * WIN * P].bitcast(BF16).rearrange("p (g w e) -> p g w e", g=GT, w=WIN)
        found = sb("found", [P, T, 5])
        counted = sb("counted", [P, T, 2])
        bad = sb("bad", [P, 4])
        general = sb("general", [P, 2])
        general_i = sb("general_i", [P, 1], I32)
        assert 5 * KP + 3 * T <= 7 * KP
        late_scratch = edge_scratch[:].bitcast(F32)
        tmp_a, tmp_b, tmp_c = (late_scratch[:, 5 * KP + i * T:5 * KP + (i + 1) * T] for i in range(3))
        all_src, all_dst, all_dst_ns, all_self = (late_scratch[:, i * KP:(i + 1) * KP] for i in range(4))
        all_src_i = edge_scratch[:, 4 * KP:5 * KP]
        slow_first = sb("slow_first", [P, 1])
        slow_idx = sb("slow_idx", [P, 1], I32)
        slow_rhs = sb("slow_rhs", [P, 2])
        counted_now = sb("counted_now", [P, 2])

        ps_agg = [psum("ps_agg0"), psum("ps_agg1")]
        ps_turn = [psum("ps_turn0"), psum("ps_turn1")]
        ps_out = [psum("ps_out0"), psum("ps_out1")]
        ps_prep = [psum("ps_prep0"), psum("ps_prep1")]

        iotas_made = sem("iotas_made")
        pads_set = sem("pads_set")
        edges_loaded = sem("edges_loaded")
        weights_loaded = sem("weights_loaded")
        prep_dve = sem("prep_dve")
        counts_ready = sem("counts_ready")
        bases_ready = sem("bases_ready")
        small_ready = sem("small_ready")
        rows_written = sem("rows_written")
        rows_loaded = sem("rows_loaded")
        edges_ready = sem("edges_ready")
        edges_stored = sem("edges_stored")
        lo_ready = sem("lo_ready")
        window_loaded = sem("window_loaded")
        window_ready = sem("window_ready")
        win_turned = sem("win_turned")
        win_copied = sem("win_copied")
        bad_ready = sem("bad_ready")
        bad_summed = sem("bad_summed")
        flag_ready = sem("flag_ready")
        hits_ready = sem("hits_ready")
        facts_summed = sem("facts_summed")
        facts_copied = sem("facts_copied")
        ends_ready = sem("ends_ready")
        ends_summed = sem("ends_summed")
        counts_final = sem("counts_final")
        degrees_ready = sem("degrees_ready")
        table_ready = sem("table_ready")
        slow_mm_wanted = sem("slow_mm_wanted")
        slow_mm_done = sem("slow_mm_done")
        slow_dve = sem("slow_dve")
        slow_pool = sem("slow_pool")
        slow_gathered = sem("slow_gathered")
        slow_rows_ready = sem("slow_rows_ready")
        slow_next = sem("slow_next")
        slow_sum_ready = sem("slow_sum_ready")
        slow_stored = sem("slow_stored")
        slow_sum_free = sem("slow_sum_free")
        slow_turned = sem("slow_turned")
        slow_turn_copied = sem("slow_turn_copied")
        x_loaded = [sem(f"x_loaded{i}") for i in range(4)]
        own_loaded = [sem(f"own_loaded{i}") for i in range(ST // 2)]
        resid_loaded = [sem("resid_loaded0"), sem("resid_loaded1")]
        rows_stored = [sem("rows_stored0"), sem("rows_stored1")]
        normed_stored = [sem("normed_stored0"), sem("normed_stored1")]
        gathered = [sem(f"gathered{j}") for j in range(ST)]
        gather_issued = sem("gather_issued")
        idx_copied = sem("idx_copied")
        scal_ready = sem("scal_ready")
        pick_ready = sem("pick_ready")
        self_ready = sem("self_ready")
        agg_done = sem("agg_done")
        combined = sem("combined")
        turn_done = sem("turn_done")
        turned_ready = sem("turned_ready")
        low_ready = sem("low_ready")
        weights_split = sem("weights_split")
        product_done = sem("product_done")
        out_read = sem("out_read")
        bias_added = sem("bias_added")
        relu_done = sem("relu_done")
        out_ready = sem("out_ready")
        stats_ready = sem("stats_ready")
        pool_step = sem("pool_step")
        ln_ready = sem("ln_ready")
        ln_applied = sem("ln_applied")

        def last_rows(h):
            return min(max(N - (NS - 1) * ST * P - h * GT * P, 0), GT * P)

        def last_dmas(h):
            r = last_rows(h)
            return (r >= P) + (r % P > 0)

        def group_of(rows, s, h):
            return rows[ds(s * (ST * P) + h * GT * P, GT * P), :].rearrange("(j p) d -> p j d", p=P)

        def short_group(rows, h):
            at, r = ((NS - 1) * ST + h * GT) * P, last_rows(h)
            full, rest = r // P, r % P
            pieces = []
            if full:
                pieces.append((rows[at:at + full * P, :].rearrange("(j p) d -> p j d", p=P), (0, full), P))
            if rest:
                pieces.append((rows[at + full * P:at + r, :].rearrange("(j p) d -> p j d", j=1), (full, full + 1), rest))
            return pieces

        def pair_of(rows, s, i):
            return rows[ds(s * (ST * P) + i * 2 * P, 2 * P), :].rearrange("(j p) d -> p j d", p=P)

        def own_count(layer, s):
            return (layer - 1) * NS * 16 + (s + 1) * 16

        def x_buffer(slot):
            return own[:, slot] if slot < 2 else neigh[:, (slot - 2) * GT:(slot - 1) * GT]

        def x_count(s, turn, h):
            n = (turn + 1) * 16
            if isinstance(s, int) and s == NS - 1:
                n = n + (last_dmas(h) - 1) * 16
            return n

        def phase0_steps(eng):
            turns = (NS - 3) // 2
            yield 0, 0, 0
            yield 1, 0, 2
            if turns:
                with eng.Fori(1, 1 + turns) as turn:
                    yield turn * 2, turn, 0
                    yield turn * 2 + 1, turn, 2
            for s in range(2 + 2 * turns, NS):
                yield s, s // 2, s % 2 * 2

        def resid_count(layer, s, h):
            n = (NS if layer == 4 else 0) * 16 + (s + 1) * 16
            if layer == 4 or (isinstance(s, int) and s == NS - 1):
                n = n + (last_dmas(h) - 1) * 16
            return n

        def pairs_done(layer, s, j):
            return (layer - 1) * (T // 2) + s * (ST // 2) + (j + 1) // 2

        def super_groups(eng):
            yield 0
            with eng.Fori(1, NS) as s:
                yield s

        def super_groups_last(eng):
            yield 0
            with eng.Fori(1, NS - 1) as s:
                yield s
            yield NS - 1

        def tile_steps(eng, ahead, first):
            for j in range(-ahead, ST if first else 0):
                yield 0, j
            with eng.Fori(1 if first else 0, NS - 1) as s:
                for j in range(ST):
                    yield s, j
            for j in range(ST):
                yield NS - 1, j

        def at(s, j, k):
            if j + k < 0 or (isinstance(s, int) and s == NS - 1 and j + k >= ST):
                return None
            i = j + k
            return s + i // ST, i % ST

        def wait_free(eng, semaphore, value):
            if not (isinstance(value, int) and value <= 0):
                eng.wait_ge(semaphore, value)

        edge_pieces = []
        for pair, shift in (((src_i, src), 0), ((dst_i, dst), 0), ((prev_i, dst), 1)):
            for b in range(KB):
                first, row = b * P * P - shift, 0
                if first < 0:
                    edge_pieces.append((pair, (0, 1), 0, 0, P - shift, shift))
                    first, row = P - shift, 1
                full = min(P - row, max(E - first, 0) // P)
                if full:
                    edge_pieces.append((pair, (row, row + full), first, b, P, 0))
                rest = min(E - first - full * P, P)
                if row + full < P and rest > 0:
                    edge_pieces.append((pair, (row + full, row + full + 1), first + full * P, b, rest, 0))

        block = ctx.enter_context(nc.Block())

        @block.sync
        def _(sp):
            sp.wait_ge(pads_set, 1)
            for flat, rows, first, b, width, skip in edge_pieces:
                n = width if rows[1] - rows[0] == 1 else P
                count = (rows[1] - rows[0] - 1) * P + n
                sp.dma_start(flat[0][rows[0]:rows[1], b, skip:skip + n],
                             flat[1][first:first + count].rearrange("(p e) -> p e", e=n)).then_inc(edges_loaded, 16)
            sp.wait_ge(small_ready, 1)
            with nc.allow_non_contiguous_dma("a few values for each chunk"):
                sp.dma_start(chunk_rows.rearrange("c (b p) -> p c b", p=P), small[:]).then_inc(rows_written, 16)
            sp.wait_ge(rows_written, 16)
            sp.dma_start(chunk_row.rearrange("p c k -> p (c k)"),
                         chunk_rows.rearrange("c k -> (c k)").partition_broadcast(P)).then_inc(rows_loaded, 16)
            sp.wait_ge(edges_ready, 1)
            sp.dma_start(edge_table.rearrange("(b p) f -> p b f", p=P),
                         edges.rearrange("p b c e -> p b (c e)")).then_inc(edges_stored, 16)

            for s, turn, slot in phase0_steps(sp):
                for h in range(2):
                    wait_free(sp, ln_applied, (s * 2 + h - 3) * GT)
                    rows_now = x_buffer(slot + h)
                    if isinstance(s, int) and s == NS - 1:
                        for rows, (t0, t1), parts in short_group(x, h):
                            sp.dma_start(rows_now[0:parts, t0:t1], rows).then_inc(x_loaded[slot + h], 16)
                    else:
                        sp.dma_start(rows_now, group_of(x, s, h)).then_inc(x_loaded[slot + h], 16)
                if isinstance(s, int) and s == 1:
                    sp.wait_ge(win_turned, 4 * WIN)
                    mats = [gcn_w[0], gcn_w[1], res_w, sage1_l, sage1_r, sage2_l, sage2_r]
                    for i, m in enumerate(mats):
                        sp.dma_start(weights[:, i], m.rearrange("(c p) n -> p c n", p=P)).then_inc(weights_loaded, 16)
                    biases = [gcn_b[0], gcn_b[1], sage1_b, sage2_b]
                    for i, v in enumerate(biases):
                        sp.dma_start(bias[:, i], v.partition_broadcast(P)).then_inc(weights_loaded, 16)
                    sp.dma_start(res_bias[:], res_b.partition_broadcast(P)).then_inc(weights_loaded, 16)

            for layer in range(1, 5):
                base = (layer - 1) * T
                if layer in (1, 3):
                    for h in range(2):
                        sp.wait_ge(normed_stored[h], 16 * NS * (1 if layer == 1 else 2))
                else:
                    for h in range(2):
                        sp.wait_ge(rows_stored[h], 16 * NS * (layer - 1))
                def load_resid(s, h):
                    if layer == 2:
                        wait_free(sp, out_ready, (s * 2 + h - 1) * (GT // 2))
                    elif not (isinstance(s, int) and s == 0):
                        sp.wait_ge(out_read, 3 * (T // 2) + (s * 2 + h - 1) * (GT // 2))
                    if layer == 4:
                        sp.dma_start(resid[:, h], group_of(x2_rows, s, h)).then_inc(resid_loaded[h], 16)
                    elif isinstance(s, int) and s == NS - 1:
                        for rows, (t0, t1), parts in short_group(x, h):
                            sp.dma_start(resid[0:parts, h, t0:t1], rows).then_inc(resid_loaded[h], 16)
                    else:
                        sp.dma_start(resid[:, h], group_of(x, s, h)).then_inc(resid_loaded[h], 16)

                for s in super_groups_last(sp):
                    for i in range(ST // 2):
                        if not (isinstance(s, int) and s == 0):
                            sp.wait_ge(turn_done, base + s * ST + i * 2 - (ST - 2))
                            sp.wait_ge(self_ready, base + s * ST + i * 2 - (ST - 2))
                        sp.dma_start(own[:, i // 2, i % 2 * 2:i % 2 * 2 + 2],
                                     pair_of(node_rows[layer - 1], s, i)).then_inc(own_loaded[i], 16)
                        if layer in (2, 4):
                            if i == 2:
                                load_resid(s, 0)
                            elif i == 0 and not (isinstance(s, int) and s == 0):
                                load_resid(s - 1, 1)
                if layer in (2, 4):
                    load_resid(NS - 1, 1)

        @block.gpsimd
        def _(pool):
            nc.gpsimd.iota(iota_i[:], [[1, P]], base=0, channel_multiplier=0)
            nc.gpsimd.iota(part_i[:], [[0, 1]], base=0, channel_multiplier=1)
            nc.gpsimd.iota(first_i[:], [[P, TW]], base=0, channel_multiplier=0)
            nc.gpsimd.iota(my_first_i[:], [[P * P, TB]], base=0, channel_multiplier=P).then_inc(iotas_made, 1)

            pool.wait_ge(edges_stored, 16)
            pool.wait_ge(lo_ready, 1)
            for tb in range(TB):
                for w in range(WIN):
                    pool.indirect_dma_start(
                        out=window[:, tb, w], out_offset=None, in_=edge_table,
                        in_offset=bass.IndirectOffsetOnAxis(ap=lo_i[:, w, tb:tb + 1], axis=0),
                        bounds_check=KP - 1, oob_is_err=False).then_inc(window_loaded, 16)

            def step(ins):
                ins.then_inc(pool_step, 1)
                pool.wait_ge(pool_step, 1)
                pool.sem_clear(pool_step)

            G = nc.gpsimd

            def ln_coefs(s, h, base, slot):
                q = base + s * 2 + h
                if not (base == 0 and isinstance(s, int) and s == 0):
                    pool.wait_ge(ln_applied, (q - 1) * GT)
                if base == 0:
                    pool.wait_ge(facts_copied, q + 1)
                pool.wait_ge(stats_ready, q + 1)
                even, odd = stat6[:, slot, :, 1:3], stat6[:, slot, :, 4:6]
                mean, var, diff = (ln_sum[:, h, :, i] for i in range(3))
                G.tensor_tensor(ln_sum[:, h, :, 0:2], even, odd, ALU.add)
                ins = G.tensor_tensor(diff, even[:, :, 0], odd[:, :, 0], ALU.subtract)
                if base == 0:
                    nodes = ds(s * ST + h * GT, GT)
                    ins = G.tensor_tensor(ln_base[:, h, 1], found[:, nodes, 0], found[:, nodes, 1], ALU.add)
                step(ins)
                ins = G.tensor_tensor(ln_sum[:, h], ln_sum[:, h], ln_factor[:], ALU.mult)
                if base == 0:
                    ins = G.tensor_tensor(ln_base[:, h, 1], ln_base[:, h, 1], counted[:, nodes, 0], ALU.add)
                step(ins)
                G.tensor_scalar(var, var, EPS, None, ALU.add)
                step(G.tensor_tensor(diff, diff, diff, ALU.mult))
                step(G.tensor_tensor(ln_base[:, h, 0], diff, var, ALU.add))
                if base == 0:
                    step(G.tensor_tensor(ln_root[:, h], ln_base[:, h], power[:], ALU.pow))
                    G.tensor_copy(table[:, nodes, DIS], ln_root[:, h, 1]).then_inc(degrees_ready, 1)
                    step(G.tensor_tensor(ln_scale[:, h], ln_root[:, h, 0], ln_root[:, h, 1], ALU.mult))
                else:
                    step(G.tensor_tensor(ln_scale[:, h], ln_base[:, h, 0], power[:, 0], ALU.pow))
                G.tensor_tensor(ln_shift[:, h], mean, ln_scale[:, h], ALU.mult).then_inc(ln_ready, 1)

            pool.wait_ge(counts_final, 1)
            for s, turn, slot in phase0_steps(pool):
                for h in range(2):
                    ln_coefs(s, h, 0, slot + h)

            pool.wait_ge(flag_ready, 1)
            is_general = pool.value_load(general_i[0:1, 0:1], min_val=0, max_val=1)
            pool.wait_ge(table_ready, 1)

            def settle(semaphore):
                pool.wait_ge(semaphore, 16)
                pool.dma_reset(range(semaphore.num, semaphore.num + 1))
                pool.sem_clear(semaphore)

            def add_bias(s, h):
                pool.wait_ge(resid_loaded[h], resid_count(4, s, h))
                G.tensor_tensor(resid[:, h], resid[:, h], bias[:, 3].unsqueeze(1).to_broadcast([P, GT, D]),
                                ALU.add).then_inc(bias_added, 1)

            def gather_slots(layer, rows):
                base = (layer - 1) * T
                for s in super_groups(pool):
                    for h in range(2):
                        wait_free(pool, gather_issued, base + (s * 2 + h - 1) * GT)
                        if not (isinstance(s, int) and s == 0):
                            pool.wait_ge(agg_done, base + (s * 2 + h - 1) * GT)
                        nc.gpsimd.tensor_copy(idx_now[:, h], src_row[:, ds(s * ST + h * GT, GT)]).then_inc(idx_copied, 1)
                        pool.wait_ge(idx_copied, 1)
                        pool.sem_clear(idx_copied)
                        for g in range(GT):
                            j = h * GT + g
                            pool.indirect_dma_start(
                                out=neigh[:, j], out_offset=None, in_=rows,
                                in_offset=bass.IndirectOffsetOnAxis(ap=idx_now[:, h, g:g + 1], axis=0),
                                bounds_check=NP - 1, oob_is_err=False, engine_sem=gather_issued).then_inc(gathered[j], 16)
                        if layer == 4:
                            if h == 1:
                                add_bias(s, 0)
                            elif not (isinstance(s, int) and s == 0):
                                add_bias(s - 1, 1)
                        if layer == 2 and not (isinstance(s, int) and s == 0):
                            ln_coefs(s - 1, h, NQ, h)
                if layer == 2:
                    for h in range(2):
                        ln_coefs(NS - 1, h, NQ, h)
                if layer == 4:
                    add_bias(NS - 1, 1)

            for layer in range(1, 5):
                base = (layer - 1) * T
                rows = node_rows[layer - 1]
                for h in range(2):
                    if layer in (1, 3):
                        pool.wait_ge(normed_stored[h], 16 * NS * (1 if layer == 1 else 2))
                    else:
                        pool.wait_ge(rows_stored[h], 16 * NS * (layer - 1))
                with pool.If(is_general):
                    with pool.Fori(0, T) as t:
                        with pool.Fori(0, K) as k:
                            nc.gpsimd.tensor_copy(slow_idx[:], all_src_i[:, ds(k, 1)]).then_inc(slow_pool, 1)
                            pool.wait_ge(slow_pool, 1)
                            pool.sem_clear(slow_pool)
                            pool.indirect_dma_start(
                                out=neigh[:, 0], out_offset=None, in_=rows,
                                in_offset=bass.IndirectOffsetOnAxis(ap=slow_idx[:], axis=0),
                                bounds_check=NP - 1, oob_is_err=False).then_inc(slow_gathered, 16)
                            settle(slow_gathered)
                            pool.sem_inc(slow_rows_ready, 1)
                            pool.wait_ge(slow_next, 1)
                            pool.sem_clear(slow_next)
                        pool.wait_ge(slow_sum_ready, 1)
                        pool.sem_clear(slow_sum_ready)
                        pool.dma_start(sum_rows[ds(t * P, P), :], done_rows[:, 0, 0]).then_inc(slow_stored, 16)
                        settle(slow_stored)
                        pool.sem_inc(slow_sum_free, 1)
                    gather_slots(layer, sum_rows)
                with pool.Else():
                    gather_slots(layer, rows)

        @block.vector
        def _(dve):
            n_links = [0]

            def link(ins):
                n_links[0] += 1
                ins.then_inc(prep_dve, 1)
                dve.wait_ge(prep_dve, n_links[0])

            V = nc.vector

            def handshake(semaphore):
                dve.wait_ge(semaphore, 1)
                dve.sem_clear(semaphore)

            def general_counts():
                for i in range(3 * KB):
                    a, b = i // KB, i % KB
                    dve.wait_ge(slow_turned, i + 1)
                    V.tensor_copy([all_src, all_dst, all_self][a][:, b * P:(b + 1) * P],
                                  ps_prep[i % 2][:, 0:P]).then_inc(slow_turn_copied, 1)
                dve.wait_ge(slow_turn_copied, 3 * KB)
                V.scalar_tensor_tensor(out=all_dst_ns, in0=all_dst, scalar=1.0, in1=all_self,
                                       op0=ALU.add, op1=ALU.mult).then_inc(slow_dve, 1)
                handshake(slow_dve)
                V.tensor_scalar(all_dst_ns, all_dst_ns, 1.0, None, ALU.subtract)
                V.tensor_scalar(all_self, all_self, -1.0, 1.0, ALU.mult, ALU.add).then_inc(slow_dve, 1)
                handshake(slow_dve)
                V.scalar_tensor_tensor(out=all_src_i, in0=all_self, scalar=FAR, in1=all_src,
                                       op0=ALU.mult, op1=ALU.add)
                V.memset(slow_rhs[:, 0:1], 1.0).then_inc(slow_dve, 1)
                handshake(slow_dve)
                with dve.Fori(0, T) as t:
                    V.tensor_copy(slow_first[:], first_node[:, ds(t, 1)])
                    V.memset(counted_now[:], 0.0).then_inc(slow_dve, 1)
                    handshake(slow_dve)
                    with dve.Fori(0, K) as k:
                        V.tensor_copy(slow_rhs[:, 1:2], all_self[:, ds(k, 1)])
                        V.tensor_scalar(pick[:, 0], iota[:], slow_first[:, 0:1], all_dst[:, ds(k, 1)],
                                        ALU.add, ALU.is_equal).then_inc(slow_mm_wanted, 1)
                        handshake(slow_mm_done)
                        V.tensor_tensor(counted_now[:], counted_now[:], ps_prep[0][:, 0:2], ALU.add).then_inc(slow_dve, 1)
                        handshake(slow_dve)
                    V.tensor_tensor(counted[:, ds(t, 1), :], counted[:, ds(t, 1), :], counted_now[:].unsqueeze(1),
                                    ALU.add).then_inc(slow_dve, 1)
                    handshake(slow_dve)

            def general_sums(layer):
                total = done_rows[:, 0, 0]
                for h in range(2):
                    if layer > 1:
                        dve.wait_ge(rows_stored[h], 16 * NS * (layer - 1))
                with dve.Fori(0, T) as t:
                    V.tensor_copy(slow_first[:], first_node[:, ds(t, 1)])
                    V.memset(total, 0.0).then_inc(slow_dve, 1)
                    handshake(slow_dve)
                    with dve.Fori(0, K) as k:
                        handshake(slow_rows_ready)
                        V.tensor_scalar(pick[:, 0], iota[:], slow_first[:, 0:1], all_dst_ns[:, ds(k, 1)],
                                        ALU.add, ALU.is_equal).then_inc(slow_mm_wanted, 1)
                        handshake(slow_mm_done)
                        V.tensor_tensor(total, total, ps_agg[0][:, 0:D], ALU.add).then_inc(slow_dve, 1)
                        handshake(slow_dve)
                        dve.sem_inc(slow_next, 1)
                    dve.sem_inc(slow_sum_ready, 1)
                    handshake(slow_sum_free)

            V.memset(src_i, PAD)
            V.memset(dst_i, PAD)
            link(V.memset(prev_i, PAD))
            V.memset(prev_i[0:1, 0, 0:1], -1).then_inc(pads_set, 1)
            V.memset(ones[:], 1.0)
            V.memset(counted[:, :, 0], 1.0)
            V.memset(counted[:, :, 1], 0.0)
            for i, factor in enumerate((-0.5, 1.0 / D, 0.5)):
                V.memset(ln_factor[:, :, i], factor)
            V.memset(power[:], -0.5)
            dve.wait_ge(iotas_made, 1)
            V.tensor_copy(iota[:], iota_i[:])
            V.tensor_copy(iota16[:], iota_i[:])
            V.tensor_scalar(iota16_1[:], iota_i[:], 1, None, ALU.add)
            V.memset(one16[:], 1.0)
            V.tensor_copy(part[:], part_i[:])
            V.tensor_copy(first_node[:], first_i[:])
            link(V.tensor_copy(my_first[:], my_first_i[:]))
            V.tensor_scalar(my_first[:], my_first[:], float((T - 1) * P), None, ALU.min)
            V.tensor_scalar(ident[:], iota[:], part[:, 0:1], None, ALU.is_equal)
            V.tensor_scalar(before[:], iota[:], part[:, 0:1], None, ALU.is_gt)

            dve.wait_ge(edges_loaded, 16 * len(edge_pieces))
            V.tensor_copy(edges[:, :, 0], src_i)
            link(V.tensor_copy(edges[:, :, 1], dst_i))
            link(V.tensor_tensor(notself[:], edges[:, :, 0], edges[:, :, 1], ALU.not_equal))
            for b in range(KB):
                ins = V.tensor_tensor_scan(rank[:, b], ones[:], notself[:, b], 0.0, ALU.mult, ALU.add)
            link(ins)
            link(V.tensor_copy(totals[:, 0], rank[:, :, P - 1]))
            V.tensor_copy(work, prev_i).then_inc(counts_ready, 1)
            V.tensor_copy(small[:, 0], edges[:, :, 1, 0])
            V.tensor_copy(small[:, 1], edges[:, :, 1, P - 1])
            dve.wait_ge(counts_ready, 1)
            link(V.tensor_tensor(lead, edges[:, :, 1], work, ALU.subtract))
            V.tensor_reduce(bad[:, 0:1], lead, AX.XY, ALU.min)
            link(V.tensor_scalar(src_i, dst_i, 7, None, ALU.arith_shift_right))
            link(V.tensor_copy(tile_of, src_i))
            link(V.tensor_scalar(src_i, prev_i, 7, None, ALU.arith_shift_right))
            link(V.tensor_copy(work, src_i))
            link(V.tensor_tensor(lead, tile_of, work, ALU.not_equal))
            dve.wait_ge(bases_ready, 1)
            V.tensor_copy(totals[:, 1], ps_prep[0][:, 0:KB])
            link(V.tensor_copy(totals[:, 2], ps_prep[0][:, KB:2 * KB]))
            link(V.tensor_tensor_scan(totals[:, 3], ones[:, 0:KB], totals[:, 2], 0.0, ALU.mult, ALU.add))
            link(V.tensor_tensor(totals[:, 3], totals[:, 3], totals[:, 2], ALU.subtract))
            link(V.tensor_tensor(totals[:, 1], totals[:, 1], totals[:, 3], ALU.add))
            for b in range(KB):
                ins = V.scalar_tensor_tensor(out=rank[:, b], in0=rank[:, b], scalar=totals[:, 1, b:b + 1], in1=notself[:, b],
                                             op0=ALU.add, op1=ALU.subtract)
            link(ins)
            link(V.tensor_tensor(work, lead, rank, ALU.mult))
            for b in range(KB):
                ins = V.tensor_tensor_scan(lead[:, b], work[:, b], work[:, b], 0.0, ALU.max, ALU.max)
            link(ins)
            V.tensor_copy(small[:, 2], lead[:, :, P - 1]).then_inc(small_ready, 1)
            V.memset(carried[:, 0:1], 0.0)
            dve.wait_ge(rows_loaded, 16)
            link(V.tensor_tensor_scan(carried[:, 1:KP + 1], chunk_row[:, 2], chunk_row[:, 2], 0.0, ALU.max, ALU.max))
            link(V.tensor_tensor(work, carried[:, 0:KP].rearrange("p (b e) -> p b e", b=KB),
                                 ident[:].unsqueeze(1).to_broadcast([P, KB, P]), ALU.mult))
            link(V.tensor_reduce(totals[:, 0], work, AX.X, ALU.add))
            for b in range(KB):
                ins = V.scalar_tensor_tensor(out=work[:, b], in0=lead[:, b], scalar=totals[:, 0, b:b + 1], in1=rank[:, b],
                                             op0=ALU.max, op1=ALU.subtract)
            link(ins)
            link(V.scalar_tensor_tensor(out=lead, in0=tile_of, scalar=float(P), in1=work,
                                        op0=ALU.mult, op1=ALU.subtract))
            link(V.scalar_tensor_tensor(out=lead, in0=lead, scalar=1.0, in1=notself[:], op0=ALU.add, op1=ALU.mult))
            V.tensor_scalar(edges[:, :, 2], lead, 1.0, None, ALU.subtract).then_inc(edges_ready, 1)
            link(V.tensor_tensor(rank, work, notself[:], ALU.mult))
            V.tensor_reduce(bad[:, 1:2], rank, AX.XY, ALU.min)
            for tb in range(TB):
                link(V.tensor_scalar(work.rearrange("p b e -> p (b e)"), chunk_row[:, 1], my_first[:, tb:tb + 1], 0.0,
                                     ALU.is_lt, ALU.add, accum_out=lo[:, 0, tb:tb + 1]))
            link(V.tensor_scalar(lo[:, 2], my_first[:], float(P), None, ALU.add))
            for tb in range(TB):
                link(V.tensor_scalar(work.rearrange("p b e -> p (b e)"), chunk_row[:, 0], lo[:, 2, tb:tb + 1], 0.0,
                                     ALU.is_lt, ALU.add, accum_out=lo[:, 1, tb:tb + 1]))
            link(V.tensor_tensor(lo[:, 1], lo[:, 1], lo[:, 0], ALU.subtract))
            V.tensor_reduce(bad[:, 2:3], lo[:, 1], AX.X, ALU.max)
            link(V.tensor_scalar(lo[:, 0], lo[:, 0], float(KP - WIN), None, ALU.min))
            for w in range(WIN):
                ins = V.tensor_scalar(lo_i[:, w], lo[:, 0], float(w), None, ALU.add)
            ins.then_inc(lo_ready, 1)
            link(V.tensor_scalar(bad[:, 0:1], bad[:, 0:1], 0.0, None, ALU.is_lt))
            link(V.tensor_scalar(bad[:, 1:2], bad[:, 1:2], float(1 - P), None, ALU.is_lt))
            link(V.tensor_scalar(bad[:, 2:3], bad[:, 2:3], float(WIN), None, ALU.is_gt))
            V.tensor_reduce(bad[:, 3:4], bad[:, 0:3], AX.X, ALU.add).then_inc(bad_ready, 1)
            dve.wait_ge(bad_summed, 1)
            link(V.tensor_scalar(general[:, 0:1], ps_prep[1][:, 0:1], 0.0, None, ALU.is_gt))
            link(V.tensor_scalar(general[:, 1:2], general[:, 0:1], -1.0, 1.0, ALU.mult, ALU.add))
            V.tensor_copy(general_i[:], general[:, 0:1]).then_inc(flag_ready, 1)

            dve.wait_ge(window_loaded, 16 * TB * WIN)
            win = window.rearrange("p t w (c e) -> p t w c e", c=3)
            for tb in range(TB):
                V.tensor_tensor(own_loop[:, tb], win[:, tb, :, 0], win[:, tb, :, 1], ALU.is_equal)
            for tb in range(TB):
                for c in (1, 2):
                    ins = V.tensor_scalar(win[:, tb, :, c], win[:, tb, :, c], my_first[:, tb:tb + 1], None, ALU.subtract)
            ins.then_inc(window_ready, 1)
            for i in range(4 * WIN):
                a, w = i // WIN, i % WIN
                dve.wait_ge(win_turned, i + 1)
                V.tensor_copy(win_t[:, a, w], ps_prep[i % 2][:, 0:TW]).then_inc(win_copied, 1)
            dve.wait_ge(win_copied, 4 * WIN)
            link(V.tensor_copy(win_i, win_t[:, 2]))
            link(V.tensor_scalar(win_j, win_i, 8, None, ALU.arith_shift_right))
            link(V.tensor_copy(facts[:, :, :, 1], win_j))
            link(V.tensor_scalar(win_j, win_i, 255, None, ALU.bitwise_and))
            V.tensor_copy(facts[:, :, :, 2], win_j)
            V.tensor_copy(facts[:, :, :, 0], win_t[:, 3])
            link(V.tensor_scalar(facts[:, :, :, 3], win_t[:, 0], 1.0, None, ALU.add))
            target, key, self_loop = win_t[:, 0], win_t[:, 1], win_t[:, 3]
            link(V.tensor_tensor(target, target, key, ALU.subtract))
            link(V.tensor_tensor(target, target, self_loop, ALU.mult))
            link(V.tensor_tensor(key, key, target, ALU.add))
            link(V.tensor_scalar(target, self_loop, -1.0, 1.0, ALU.mult, ALU.add))
            for f in (1, 2, 3):
                ins = V.tensor_tensor(facts[:, :, :, f], facts[:, :, :, f], target, ALU.mult)
            link(ins)

            dve.wait_ge(flag_ready, 1)
            is_general = dve.value_load(general_i[0:1, 0:1], min_val=0, max_val=1)
            with dve.If(is_general):
                general_counts()
            dve.sem_inc(counts_final, 1)

            def find_ends(s, h):
                dve.wait_ge(facts_summed, (s * 2 + h + 1) * GT)
                wait_free(dve, ends_summed, s * 2 + h - 1)
                targets = ps_prep[h][:, 0:GT * 4].rearrange("p (g f) -> p g f", f=4)[:, :, 3:4]
                V.tensor_tensor(ends[:, h], iota16_1[:].unsqueeze(1).to_broadcast([P, GT, P]),
                                targets.to_broadcast([P, GT, P]), ALU.is_equal).then_inc(ends_ready, 1)

            for s, turn, slot in phase0_steps(dve):
                for h in range(2):
                    wait_free(dve, facts_summed, (s * 2 + h - 1) * GT)
                    V.tensor_copy(key_now[:, h], win_t[:, 1, :, ds(s * ST + h * GT, GT)])
                    V.tensor_copy(facts_now[:, h], facts[:, :, ds(s * ST + h * GT, GT), :]).then_inc(hits_ready, 1)
                    dve.wait_ge(hits_ready, (s * 2 + h) * (GT + 1) + 1)
                    for g in range(GT):
                        wait_free(dve, facts_summed, s * ST + h * GT + g - 3)
                        V.tensor_tensor(hits[:, g], iota16[:].unsqueeze(1).to_broadcast([P, WIN, P]),
                                        key_now[:, h, :, g:g + 1].to_broadcast([P, WIN, P]),
                                        ALU.is_equal).then_inc(hits_ready, 1)
                    if h == 1:
                        find_ends(s, 0)
                    elif not (isinstance(s, int) and s == 0):
                        find_ends(s - 1, 1)
                    dve.wait_ge(x_loaded[slot + h], x_count(s, turn, h))
                    wait_free(dve, ln_ready, s * 2 + h - 3)
                    for g in range(GT):
                        ins = V.bn_stats(stat6[:, slot + h, g], x_buffer(slot + h)[:, g])
                    ins.then_inc(stats_ready, 1)

            find_ends(NS - 1, 1)

            dve.wait_ge(facts_copied, NQ)
            dve.wait_ge(degrees_ready, NQ)

            table_f = [table[:, :, f] for f in range(NF)]
            link(V.tensor_tensor(found[:, :, 0], found[:, :, 0], found[:, :, 1], ALU.add))
            link(V.tensor_tensor(found[:, :, 0:2], found[:, :, 0:2], counted[:], ALU.add))
            link(V.tensor_copy(tmp_a, found[:, :, 0]))
            link(V.tensor_scalar(found[:, :, 0], found[:, :, 0], 1.0, None, ALU.subtract))
            link(V.reciprocal(table_f[DIS2], tmp_a))
            link(V.tensor_scalar(tmp_c, found[:, :, 0], 1.0, None, ALU.max))
            link(V.reciprocal(table_f[INV], tmp_c))
            V.tensor_tensor(table_f[SELF_S], found[:, :, 1], table_f[INV], ALU.mult)
            link(V.scalar_tensor_tensor(out=table_f[SELF_G], in0=found[:, :, 1], scalar=1.0, in1=table_f[DIS2],
                                        op0=ALU.add, op1=ALU.mult))
            link(V.tensor_tensor(table_f[SQ], table_f[DIS], tmp_a, ALU.mult))
            link(V.tensor_scalar(tmp_a, found[:, :, 4], 1.0, None, ALU.subtract))
            link(V.tensor_scalar(tmp_a, tmp_a, general[:, 1:2], None, ALU.mult))
            link(V.tensor_scalar(tmp_b, general[:, 0:1].to_broadcast([P, T]), part[:, 0:1], None, ALU.mult))
            link(V.tensor_tensor(table_f[SLOT], tmp_a, tmp_b, ALU.add))
            V.tensor_scalar(tmp_c, found[:, :, 4], 0.5, FAR, ALU.is_lt, ALU.mult)
            link(V.scalar_tensor_tensor(out=tmp_a, in0=found[:, :, 2], scalar=256.0, in1=found[:, :, 3],
                                        op0=ALU.mult, op1=ALU.add))
            link(V.tensor_tensor(tmp_a, tmp_a, tmp_c, ALU.add))
            link(V.tensor_scalar(tmp_a, tmp_a, general[:, 1:2], None, ALU.mult))
            link(V.tensor_scalar(tmp_c, first_node[:, 0:T], part[:, 0:1], None, ALU.add))
            link(V.scalar_tensor_tensor(out=tmp_a, in0=tmp_c, scalar=general[:, 0:1], in1=tmp_a,
                                        op0=ALU.mult, op1=ALU.add))
            V.memset(table_f[NF - 1], 0.0)
            V.tensor_copy(src_row[:], tmp_a).then_inc(table_ready, 1)
            dve.wait_ge(table_ready, 1)
            dve.wait_ge(weights_loaded, 16 * 12)
            link(V.tensor_copy(weights_hi[:], weights))
            V.tensor_tensor(weights_lo[:], weights, weights_hi[:].bitcast(F32), ALU.subtract).then_inc(weights_split, 1)
            dve.wait_ge(weights_split, 1)
            for i in range(2):
                ins = V.tensor_tensor(bias[:, i], bias[:, i], res_bias[:], ALU.add)
            link(ins)

            for layer in range(1, 5):
                gcn = layer <= 2
                base = (layer - 1) * T
                gbase = (layer - 1) * NQ
                with dve.If(is_general):
                    general_sums(layer)
                if layer == 2:
                    K_PICK, K_SUM, K_LOW, K_OUT, K_RESID, K_STATS = 6, 5, 4, 2, 1, 0
                else:
                    K_PICK, K_SUM, K_LOW, K_OUT = 6, 5, 4, 1

                def finish_pair(s, j):
                    h, g = j // GT, j % GT
                    pair = ps_out[(j // 2) % 2]
                    if g == 1:
                        wait_free(dve, rows_stored[h], ((layer - 1) * NS + s) * 16)
                        if layer == 2 and not (isinstance(s, int) and s == 0):
                            dve.wait_ge(ln_applied, (NQ + s * 2 + h - 1) * GT)
                        if layer == 4:
                            dve.wait_ge(bias_added, s * 2 + h + 1)
                    dve.wait_ge(product_done, base + s * ST + j + 1)
                    if gcn:
                        for e in (0, 1):
                            o, p_ = done_rows[:, h, g - 1 + e], pair[:, e * D:(e + 1) * D]
                            if layer == 1:
                                ins = V.scalar_tensor_tensor(out=o, in0=bias[:, 0], scalar=scal[:, h, g - 1 + e, DIS:DIS + 1],
                                                             in1=p_, op0=ALU.mult, op1=ALU.add)
                            else:
                                ins = V.scalar_tensor_tensor(out=o, in0=p_, scalar=scal[:, h, g - 1 + e, SQ:SQ + 1],
                                                             in1=bias[:, 1], op0=ALU.mult, op1=ALU.add)
                    else:
                        o = done_rows[:, h, g - 1:g + 1]
                        p_ = pair[:].rearrange("p (a d) -> p a d", a=2)
                        other = (bias[:, 2].unsqueeze(1).to_broadcast([P, 2, D]) if layer == 3
                                 else resid[:, h, g - 1:g + 1])
                        ins = V.tensor_tensor(o, p_, other, ALU.add)
                    ins.then_inc(out_read, 1)

                def add_resid(s, j):
                    h, g = j // GT, j % GT
                    if g == 1:
                        dve.wait_ge(resid_loaded[h], resid_count(2, s, h))
                    dve.wait_ge(out_read, pairs_done(2, s, j))
                    rows = done_rows[:, h, g - 1:g + 1].rearrange("p j d -> p (j d)")
                    V.scalar_tensor_tensor(out=rows, in0=rows, scalar=0.0,
                                           in1=resid[:, h, g - 1:g + 1].rearrange("p j d -> p (j d)"),
                                           op0=ALU.max, op1=ALU.add).then_inc(out_ready, 1)

                def tile_stats(s, j):
                    h, g = j // GT, j % GT
                    if g == 0:
                        dve.wait_ge(ln_ready, NQ + s * 2 + h - 1)
                    dve.wait_ge(out_ready, pairs_done(1, s, j | 1))
                    ins = V.bn_stats(stat6[:, h, g], done_rows[:, h, g])
                    if g == GT - 1:
                        ins.then_inc(stats_ready, 1)

                for s, j in tile_steps(dve, K_PICK, layer == 1):
                    c = at(s, j, K_OUT)
                    if c and c[1] % 2 == 1:
                        finish_pair(*c)
                    c = at(s, j, K_PICK)
                    if c:
                        s_, j_ = c
                        h = j_ // GT
                        if j_ % GT == 0:
                            wait_free(dve, out_read, (layer - 1) * (T // 2) + (s_ * 2 + h - 1) * (GT // 2))
                            V.tensor_copy(scal[:, h], table[:, ds(s_ * ST + h * GT, GT), :]).then_inc(scal_ready, 1)
                            dve.wait_ge(scal_ready, gbase + s_ * 2 + h + 1)
                        wait_free(dve, agg_done, base + s_ * ST + j_ - 3)
                        V.tensor_scalar(pick[:, j_ % 4], iota[:], scal[:, h, j_ % GT, SLOT:SLOT + 1], None,
                                        ALU.is_equal).then_inc(pick_ready, 1)
                    c = at(s, j, K_SUM)
                    if c:
                        s_, j_ = c
                        n = base + s_ * ST + j_
                        f = DIS2 if gcn else INV
                        dve.wait_ge(agg_done, n + 1)
                        dve.wait_ge(self_ready, n + 1)
                        wait_free(dve, turn_done, n - 1)
                        V.scalar_tensor_tensor(out=agg[:, j_ % 2], in0=ps_agg[j_ % 2][:, 0:D],
                                               scalar=scal[:, j_ // GT, j_ % GT, f:f + 1], in1=selfpart[:, j_ % 4],
                                               op0=ALU.mult, op1=ALU.add).then_inc(combined, 1)
                    c = at(s, j, K_LOW)
                    if c:
                        s_, j_ = c
                        n = base + s_ * ST + j_
                        dve.wait_ge(turned_ready, n + 1)
                        wait_free(dve, product_done, n - 3)
                        V.tensor_tensor(turned_lo[:, j_ % 4], ps_turn[j_ % 2][:], turned_hi[:, j_ % 4].bitcast(F32),
                                        ALU.subtract).then_inc(low_ready, 1)
                    if layer == 2:
                        c = at(s, j, K_RESID)
                        if c and c[1] % 2 == 1:
                            add_resid(*c)
                        c = at(s, j, K_STATS)
                        if c:
                            tile_stats(*c)

        @block.scalar
        def _(act):
            def normalize(rows, h, tiles):
                for g in tiles:
                    nc.scalar.activation(normed[:, h, g], rows[:, g], ACT.Relu, scale=ln_scale[:, h, g:g + 1],
                                         bias=ln_shift[:, h, g:g + 1]).then_inc(ln_applied, 1)

            def store_normed(rows, base, s, h):
                act.wait_ge(ln_applied, (base + s * 2 + h + 1) * GT)
                act.dma_start(group_of(rows, s, h), normed[:, h]).then_inc(normed_stored[h], 16)

            def phase0_norm(s, h, slot):
                act.wait_ge(ln_ready, s * 2 + h + 1)
                wait_free(act, normed_stored[h], s * 16)
                normalize(x_buffer(slot), h, range(GT))
                store_normed(node_rows[0], 0, s, h)

            act.wait_ge(flag_ready, 1)
            def copy_found(s, h):
                act.wait_ge(ends_summed, s * 2 + h + 1)
                nodes = ds(s * ST + h * GT, GT)
                nc.scalar.activation(found[:, nodes, 1:5], ps_prep[h][:, 0:GT * 4].rearrange("p (g f) -> p g f", f=4),
                                     ACT.Copy, scale=general[:, 1:2])
                nc.scalar.activation(found[:, nodes, 0:1], ps_prep[h][:, GT * 4:GT * 5].unsqueeze(2),
                                     ACT.Copy, scale=general[:, 1:2]).then_inc(facts_copied, 1)

            for s, turn, slot in phase0_steps(act):
                for h in range(2):
                    at_start = isinstance(s, int) and s == 0
                    if h == 1:
                        copy_found(s, 0)
                        if not at_start:
                            phase0_norm(s - 1, 1, 3 - slot)
                    elif not at_start:
                        copy_found(s - 1, 1)
                        phase0_norm(s - 1, 0, 2 - slot)
            copy_found(NS - 1, 1)
            phase0_norm(NS - 1, 0, (NS - 1) % 2 * 2)
            phase0_norm(NS - 1, 1, (NS - 1) % 2 * 2 + 1)

            for layer in range(1, 5):
                gcn = layer <= 2
                base = (layer - 1) * T
                gbase = (layer - 1) * NQ
                K_SELF, K_TURNED, K_STORE = (8, 7, 2) if layer == 2 else (6, 5, 0)
                f = SELF_G if gcn else SELF_S

                for s, j in tile_steps(act, K_SELF, layer == 1):
                    c = at(s, j, K_SELF)
                    if c:
                        s_, j_ = c
                        h, n = j_ // GT, base + s_ * ST + j_
                        if j_ % 2 == 0:
                            act.wait_ge(own_loaded[j_ // 2], own_count(layer, s_))
                        if j_ % GT == 0:
                            act.wait_ge(scal_ready, gbase + s_ * 2 + h + 1)
                        wait_free(act, combined, n - 3)
                        nc.scalar.activation(selfpart[:, j_ % 4], own[:, h, j_ % GT], ACT.Copy,
                                             scale=scal[:, h, j_ % GT, f:f + 1]).then_inc(self_ready, 1)
                    c = at(s, j, K_TURNED)
                    if c:
                        s_, j_ = c
                        n = base + s_ * ST + j_
                        act.wait_ge(turn_done, n + 1)
                        wait_free(act, product_done, n - 3)
                        nc.scalar.copy(turned_hi[:, j_ % 4], ps_turn[j_ % 2][:]).then_inc(turned_ready, 1)
                    c = at(s, j, 1)
                    if layer in (1, 3) and c and c[1] % 2 == 1:
                        s_, h, g = c[0], c[1] // GT, c[1] % GT
                        act.wait_ge(out_read, pairs_done(layer, s_, c[1]))
                        nc.scalar.activation(done_rows[:, h, g - 1:g + 1], done_rows[:, h, g - 1:g + 1],
                                             ACT.Relu).then_inc(relu_done, 1)
                    c = at(s, j, K_STORE)
                    if c and c[1] % GT == GT - 1:
                        s_, h = c[0], c[1] // GT
                        if layer in (1, 3):
                            act.wait_ge(relu_done, pairs_done(1 if layer == 1 else 2, s_, c[1]))
                        elif layer == 2:
                            act.wait_ge(out_ready, pairs_done(1, s_, c[1]))
                        else:
                            act.wait_ge(out_read, pairs_done(layer, s_, c[1]))
                        if layer < 4:
                            rows = x2_rows if layer == 2 else node_rows[layer]
                            act.dma_start(group_of(rows, s_, h), done_rows[:, h]).then_inc(rows_stored[h], 16)
                        elif isinstance(s_, int) and s_ == NS - 1:
                            for rows, (t0, t1), parts in short_group(out, h):
                                act.dma_start(rows, done_rows[0:parts, h, t0:t1]).then_inc(rows_stored[h], 16)
                        else:
                            act.dma_start(group_of(out, s_, h), done_rows[:, h]).then_inc(rows_stored[h], 16)
                    if layer == 2:
                        for k, half in ((1, (0, 1)), (0, (2, 3))):
                            c = at(s, j, k)
                            if c and c[1] % GT == GT - 1:
                                s_, h = c[0], c[1] // GT
                                if k == 1:
                                    act.wait_ge(ln_ready, NQ + s_ * 2 + h + 1)
                                    act.wait_ge(normed_stored[h], (NS + s_) * 16)
                                normalize(done_rows[:, h], h, half)
                        c = at(s, j, 0)
                        if c and c[1] % GT == GT - 1:
                            store_normed(node_rows[2], NQ, c[0], c[1] // GT)
            for h in range(2):
                act.wait_ge(rows_stored[h], 16 * (4 * NS + last_dmas(h) - 1))
                act.wait_ge(normed_stored[h], 16 * 2 * NS)

        @block.tensor
        def _(pe):
            mm = nc.tensor.matmul
            pe.wait_ge(counts_ready, 1)
            mm(ps_prep[0][:, 0:KB], before[:], totals[:, 0], start=True, stop=True)
            mm(ps_prep[0][:, KB:2 * KB], ones[:], totals[:, 0], start=True, stop=True).then_inc(bases_ready, 1)
            pe.wait_ge(bad_ready, 1)
            mm(ps_prep[1][:, 0:1], ones[:], bad[:, 3:4], start=True, stop=True).then_inc(bad_summed, 1)
            pe.wait_ge(window_ready, 1)
            win = window.rearrange("p t w (c e) -> p t w c e", c=3)
            for i in range(4 * WIN):
                a, w = i // WIN, i % WIN
                if i >= 2:
                    pe.wait_ge(win_copied, i - 1)
                for tb in range(TB):
                    source = own_loop[:, tb, w] if a == 3 else win[:, tb, w, (1, 2, 0)[a]]
                    ins = nc.tensor.transpose(ps_prep[i % 2][:, tb * P:(tb + 1) * P], source, ident[:])
                ins.then_inc(win_turned, 1)
            pe.wait_ge(win_copied, 4 * WIN)
            pe.wait_ge(flag_ready, 1)
            is_general = pe.value_load(general_i[0:1, 0:1], min_val=0, max_val=1)
            with pe.If(is_general):
                for i in range(3 * KB):
                    a, b = i // KB, i % KB
                    if i >= 2:
                        pe.wait_ge(slow_turn_copied, i - 1)
                    source = notself[:, b] if a == 2 else edges[:, b, a]
                    nc.tensor.transpose(ps_prep[i % 2][:, 0:P], source, ident[:]).then_inc(slow_turned, 1)
                with pe.Fori(0, T) as t:
                    with pe.Fori(0, K) as k:
                        pe.wait_ge(slow_mm_wanted, 1)
                        pe.sem_clear(slow_mm_wanted)
                        mm(ps_prep[0][:, 0:2], pick[:, 0], slow_rhs[:], start=True, stop=True).then_inc(slow_mm_done, 1)

            def sum_ends(s, h):
                pe.wait_ge(ends_ready, s * 2 + h + 1)
                for g in range(GT):
                    ins = mm(ps_prep[h][:, GT * 4 + g:GT * 4 + g + 1], ends[:, h, g], one16[:], start=True, stop=True)
                ins.then_inc(ends_summed, 1)

            for s in super_groups(pe):
                for h in range(2):
                    q = s * 2 + h
                    wait_free(pe, facts_copied, q - 1)
                    for g in range(GT):
                        pe.wait_ge(hits_ready, q * (GT + 1) + g + 2)
                        for w in range(WIN):
                            ins = mm(ps_prep[h][:, g * 4:g * 4 + 4], hits[:, g, w], facts_now[:, h, w, g, :],
                                     start=(w == 0), stop=(w == WIN - 1))
                        ins.then_inc(facts_summed, 1)
                    if h == 1:
                        sum_ends(s, 0)
                    elif not (isinstance(s, int) and s == 0):
                        sum_ends(s - 1, 1)
            sum_ends(NS - 1, 1)

            pe.wait_ge(weights_split, 1)
            for layer in range(1, 5):
                base = (layer - 1) * T
                w_sum, w_own = ((0, 2), (1, 2), (3, 4), (5, 6))[layer - 1]
                with pe.If(is_general):
                    with pe.Fori(0, T) as t:
                        with pe.Fori(0, K) as k:
                            pe.wait_ge(slow_mm_wanted, 1)
                            pe.sem_clear(slow_mm_wanted)
                            mm(ps_agg[0][:, 0:D], pick[:, 0], neigh[:, 0], start=True, stop=True).then_inc(slow_mm_done, 1)
                K_AGG, K_TURN = (4, 3) if layer == 2 else (5, 4)
                for s, j in tile_steps(pe, K_AGG, layer == 1):
                    c = at(s, j, K_AGG)
                    if c:
                        s_, j_ = c
                        n = base + s_ * ST + j_
                        pe.wait_ge(pick_ready, n + 1)
                        pe.wait_ge(gathered[j_], 16 * ((layer - 1) * NS + 1 + s_))
                        wait_free(pe, combined, n - 1)
                        mm(ps_agg[j_ % 2][:, 0:D], pick[:, j_ % 4], neigh[:, j_], start=True, stop=True).then_inc(agg_done, 1)
                    c = at(s, j, K_TURN)
                    if c:
                        s_, j_ = c
                        h, n = j_ // GT, base + s_ * ST + j_
                        if j_ % 2 == 0:
                            pe.wait_ge(own_loaded[j_ // 2], own_count(layer, s_))
                        pe.wait_ge(combined, n + 1)
                        wait_free(pe, low_ready, n - 1)
                        for b in range(2 * DC):
                            source = agg[:, j_ % 2] if b < DC else own[:, h, j_ % GT]
                            ins = nc.tensor.transpose(ps_turn[j_ % 2][:, b * P:(b + 1) * P],
                                                      source[:, (b % DC) * P:(b % DC + 1) * P], ident[:])
                        ins.then_inc(turn_done, 1)
                    c = at(s, j, 2)
                    if c:
                        s_, j_ = c
                        n = base + s_ * ST + j_
                        pe.wait_ge(low_ready, n + 1)
                        if j_ % 2 == 0:
                            wait_free(pe, out_read, base // 2 + s_ * (ST // 2) + (j_ // 2 - 1))
                        o = ps_out[(j_ // 2) % 2][:, (j_ % 2) * D:(j_ % 2 + 1) * D]
                        parts = ((turned_lo, weights_hi), (turned_hi, weights_lo), (turned_hi, weights_hi))
                        for b in range(2 * DC):
                            for i, (left, right) in enumerate(parts):
                                ins = mm(o, left[:, j_ % 4, b * P:(b + 1) * P], right[:, (w_sum, w_own)[b // DC], b % DC],
                                         start=(b + i == 0), stop=(b == 2 * DC - 1 and i == 2))
                        ins.then_inc(product_done, 1)


_INS = ["x", "src", "dst", "L0_gnn_W", "L0_gnn_b", "L0_gnn_resW", "L0_gnn_resb", "L1_gnn_W1_l", "L1_gnn_W1_r",
        "L1_gnn_b1", "L1_gnn_W2_l", "L1_gnn_W2_r", "L1_gnn_b2"]


def kernel(**inputs):
    import numpy as _np
    import concourse.bacc as _bacc
    from concourse import mybir as _mybir
    from concourse.bass_utils import run_bass_kernel_spmd as _run

    nc = _bacc.Bacc("TRN2", target_bir_lowering=False, num_devices=1)
    arrays, args = {}, []
    for name in _INS:
        a = _np.ascontiguousarray(inputs[name])
        arrays[f"in_{name}_dram"] = a
        args.append(nc.dram_tensor(f"in_{name}_dram", a.shape, _mybir.dt.from_np(a.dtype), kind="ExternalInput").ap())
    shape = tuple(inputs["x"].shape)
    out = nc.dram_tensor("out_0_dram", shape, _mybir.dt.float32, kind="ExternalOutput").ap()
    gnn_kernel(nc, *args, out)
    r = _run(nc, [arrays], core_ids=[0])
    return r.results[0]["out_0_dram"]
```
